# Optimizing a Trainium2 kernel written in Bass

```python
import numpy as np
import jax
import jax.numpy as jnp

def _softmax(x, axis=-1):
    return jax.nn.softmax(x, axis=axis)

def _gelu(x):
    return jax.nn.gelu(x, approximate=True)

def _silu(x):
    return jax.nn.silu(x)

def _sigmoid(x):
    return jax.nn.sigmoid(x)

def _layernorm(x, axis=-1, eps=1e-05):
    m = jnp.mean(x, axis=axis, keepdims=True)
    v = jnp.var(x, axis=axis, keepdims=True)
    return (x - m) / jnp.sqrt(v + eps)

def _scatter_add(tgt, idx, src, axis=0):
    return tgt.at[idx].add(src)

def _segment_sum(src, seg, n):
    return jax.ops.segment_sum(src, seg, n)
kernel_name = 'mk_seq_postln_d2_jaxref_r4_2a3e0e'

def setup_inputs(seed: int=0):
    np.random.seed(seed)
    _w = jnp.asarray

    def _L0_attn_setup():
        import jax, jax.numpy as jnp
        import numpy as np
        N_HEADS = 16
        ROPE_BASE = 10000.0

        def _rotate_every_two(x):
            x_even = x[..., ::2]
            x_odd = x[..., 1::2]
            return jnp.stack((-x_odd, x_even), axis=-1).reshape(x.shape)

        def _rope_cos_sin(seq_len, head_dim):
            inv_freq = 1.0 / ROPE_BASE ** (jnp.arange(0, head_dim, 2, dtype=jnp.float32) / head_dim)
            pos = jnp.arange(seq_len, dtype=jnp.float32)
            freqs = pos[:, None] * inv_freq[None, :]
            emb = jnp.repeat(freqs, 2, axis=-1)
            return (jnp.cos(emb)[None, None], jnp.sin(emb)[None, None])
        key = jax.random.key(seed)
        ks = jax.random.split(key, 5)
        B, S, D = (2, 512, 256)
        std = 0.02
        return {'x': jax.random.normal(ks[0], (B, S, D), dtype=jnp.float32), 'Wq': jax.random.normal(ks[1], (D, D), dtype=jnp.float32) * std, 'Wk': jax.random.normal(ks[2], (D, D), dtype=jnp.float32) * std, 'Wv': jax.random.normal(ks[3], (D, D), dtype=jnp.float32) * std, 'Wo': jax.random.normal(ks[4], (D, D), dtype=jnp.float32) * std}
    _L0_attn_in = _L0_attn_setup()

    def _L0_ffn_setup():
        import jax, jax.numpy as jnp
        import numpy as np
        B, T, E, C, H, G = (2, 512, 8, 256, 512, 16)
        key = jax.random.key(seed)
        ks = jax.random.split(key, 7)
        return {'hidden_states': jax.random.normal(ks[0], (B, T, C), jnp.float32), 'w_red': jax.random.normal(ks[1], (C, G), jnp.float32) * 0.02, 'wg': jax.random.normal(ks[2], (E, G), jnp.float32), 'W1': jax.random.normal(ks[3], (E, C, H), jnp.float32) * 0.02, 'b1': jax.random.normal(ks[4], (E, H), jnp.float32) * 0.02, 'W2': jax.random.normal(ks[5], (E, H, C), jnp.float32) * 0.02, 'b2': jax.random.normal(ks[6], (E, C), jnp.float32) * 0.02}
    _L0_ffn_in = _L0_ffn_setup()

    def _L1_attn_setup():
        import jax, jax.numpy as jnp
        import numpy as np
        D_MODEL = 256
        N_HEADS = 16
        HEAD_DIM = D_MODEL // N_HEADS
        WINDOW = 128
        LOCAL_BLOCK = 64
        LATENT_TOKENS = 64
        LATENT_D = 64
        LATENT_HEADS = 4
        LATENT_HD = LATENT_D // LATENT_HEADS
        NEG = -1000000000.0

        def _local_attention(q, k, v):
            B, H, S, hd = q.shape
            bs = min(S, max(WINDOW, LOCAL_BLOCK))
            nb = S // bs
            w = WINDOW
            L = bs + w - 1
            k_pad = jnp.pad(k, ((0, 0), (0, 0), (w - 1, 0), (0, 0)))
            v_pad = jnp.pad(v, ((0, 0), (0, 0), (w - 1, 0), (0, 0)))
            starts = jnp.arange(nb) * bs
            idx = starts[:, None] + jnp.arange(L)[None, :]
            kb = k_pad[:, :, idx]
            vb = v_pad[:, :, idx]
            qb = q.reshape(B, H, nb, bs, hd)
            q_pos = starts[:, None] + jnp.arange(bs)[None, :]
            k_gpos = starts[:, None] + jnp.arange(L)[None, :] - (w - 1)
            dist = q_pos[:, :, None] - k_gpos[:, None, :]
            allowed = (dist > 0) & (dist <= w) & (k_gpos[:, None, :] >= 0)
            scale = 1.0 / np.sqrt(hd)
            scores = jnp.einsum('bhnqd,bhnkd->bhnqk', qb, kb) * scale
            scores = jnp.where(allowed, scores, NEG)
            attn = jax.nn.softmax(scores, axis=-1)
            attn = jnp.where(allowed.any(-1)[None, None, :, :, None], attn, 0.0)
            out = jnp.einsum('bhnqk,bhnkd->bhnqd', attn, vb)
            return out.reshape(B, H, S, hd)
        key = jax.random.key(seed)
        ks = jax.random.split(key, 14)
        B, S = (2, 1024)
        s = 0.02
        f32 = jnp.float32
        return {'x': jax.random.normal(ks[0], (B, S, D_MODEL), f32), 'qkv_w': jax.random.normal(ks[1], (D_MODEL, 3 * D_MODEL), f32) * s, 'qkv_b': jnp.zeros((3 * D_MODEL,), f32), 'rq_w': jax.random.normal(ks[2], (D_MODEL, LATENT_D), f32) * s, 'rq_b': jnp.zeros((LATENT_D,), f32), 'rkv_w': jax.random.normal(ks[3], (D_MODEL, 2 * LATENT_D), f32) * s, 'rkv_b': jnp.zeros((2 * LATENT_D,), f32), 'rout_w': jax.random.normal(ks[4], (LATENT_D, D_MODEL), f32) * s, 'rout_b': jnp.zeros((D_MODEL,), f32), 'out_w': jax.random.normal(ks[5], (D_MODEL, D_MODEL), f32) * s, 'out_b': jnp.zeros((D_MODEL,), f32), 'gl_w': jax.random.normal(ks[6], (HEAD_DIM, 1), f32) * s, 'gr_w': jax.random.normal(ks[7], (HEAD_DIM, 1), f32) * s}
    _L1_attn_in = _L1_attn_setup()

    def _L1_ffn_setup():
        import jax, jax.numpy as jnp
        import numpy as np
        B, S, D, H, E = (64, 256, 256, 64, 8)
        EPS = 1e-05
        key = jax.random.key(seed)
        ks = jax.random.split(key, 8)
        x = jax.random.normal(ks[0], (B, S, D), jnp.float32)
        return {'x': x, 'ln_g': jnp.ones((D,), jnp.float32), 'ln_b': jnp.zeros((D,), jnp.float32), 'bn_g': jnp.ones((D,), jnp.float32), 'bn_b': jnp.zeros((D,), jnp.float32), 'bn_mean': jax.random.normal(ks[1], (D,), jnp.float32) * 0.01, 'bn_var': jnp.ones((D,), jnp.float32), 'Wr': jax.random.normal(ks[2], (D, E), jnp.float32) * 0.02, 'br': jnp.zeros((E,), jnp.float32), 'W_down': jax.random.normal(ks[3], (E, D, H), jnp.float32) * 0.02, 'b_down': jnp.zeros((E, H), jnp.float32), 'W_up': jax.random.normal(ks[4], (E, H, D), jnp.float32) * 0.02, 'b_up': jnp.zeros((E, D), jnp.float32)}
    _L1_ffn_in = _L1_ffn_setup()
    _d = {'L0_attn_x': _L0_attn_in['x'], 'L0_attn_Wq': _L0_attn_in['Wq'], 'L0_attn_Wk': _L0_attn_in['Wk'], 'L0_attn_Wv': _L0_attn_in['Wv'], 'L0_attn_Wo': _L0_attn_in['Wo'], 'L0_ffn_w_red': _L0_ffn_in['w_red'], 'L0_ffn_wg': _L0_ffn_in['wg'], 'L0_ffn_W1': _L0_ffn_in['W1'], 'L0_ffn_b1': _L0_ffn_in['b1'], 'L0_ffn_W2': _L0_ffn_in['W2'], 'L0_ffn_b2': _L0_ffn_in['b2'], 'L1_attn_qkv_w': _L1_attn_in['qkv_w'], 'L1_attn_qkv_b': _L1_attn_in['qkv_b'], 'L1_attn_rq_w': _L1_attn_in['rq_w'], 'L1_attn_rq_b': _L1_attn_in['rq_b'], 'L1_attn_rkv_w': _L1_attn_in['rkv_w'], 'L1_attn_rkv_b': _L1_attn_in['rkv_b'], 'L1_attn_rout_w': _L1_attn_in['rout_w'], 'L1_attn_rout_b': _L1_attn_in['rout_b'], 'L1_attn_out_w': _L1_attn_in['out_w'], 'L1_attn_out_b': _L1_attn_in['out_b'], 'L1_attn_gl_w': _L1_attn_in['gl_w'], 'L1_attn_gr_w': _L1_attn_in['gr_w'], 'L1_ffn_ln_g': _L1_ffn_in['ln_g'], 'L1_ffn_ln_b': _L1_ffn_in['ln_b'], 'L1_ffn_bn_g': _L1_ffn_in['bn_g'], 'L1_ffn_bn_b': _L1_ffn_in['bn_b'], 'L1_ffn_bn_mean': _L1_ffn_in['bn_mean'], 'L1_ffn_bn_var': _L1_ffn_in['bn_var'], 'L1_ffn_Wr': _L1_ffn_in['Wr'], 'L1_ffn_br': _L1_ffn_in['br'], 'L1_ffn_W_down': _L1_ffn_in['W_down'], 'L1_ffn_b_down': _L1_ffn_in['b_down'], 'L1_ffn_W_up': _L1_ffn_in['W_up'], 'L1_ffn_b_up': _L1_ffn_in['b_up']}
    _x0 = _d['L0_attn_x']
    _d['L0_attn_x'] = jax.random.normal(jax.random.fold_in(jax.random.key(seed), 1), (8, 512, 256), dtype=_x0.dtype)
    del _x0
    return _d

def reference(L0_attn_x, L0_attn_Wq, L0_attn_Wk, L0_attn_Wv, L0_attn_Wo, L0_ffn_w_red, L0_ffn_wg, L0_ffn_W1, L0_ffn_b1, L0_ffn_W2, L0_ffn_b2, L1_attn_qkv_w, L1_attn_qkv_b, L1_attn_rq_w, L1_attn_rq_b, L1_attn_rkv_w, L1_attn_rkv_b, L1_attn_rout_w, L1_attn_rout_b, L1_attn_out_w, L1_attn_out_b, L1_attn_gl_w, L1_attn_gr_w, L1_ffn_ln_g, L1_ffn_ln_b, L1_ffn_bn_g, L1_ffn_bn_b, L1_ffn_bn_mean, L1_ffn_bn_var, L1_ffn_Wr, L1_ffn_br, L1_ffn_W_down, L1_ffn_b_down, L1_ffn_W_up, L1_ffn_b_up):

    def _L0_attn_ref(x, Wq, Wk, Wv, Wo):
        import jax, jax.numpy as jnp
        import numpy as np
        N_HEADS = 16
        ROPE_BASE = 10000.0

        def _rotate_every_two(x):
            x_even = x[..., ::2]
            x_odd = x[..., 1::2]
            return jnp.stack((-x_odd, x_even), axis=-1).reshape(x.shape)

        def _rope_cos_sin(seq_len, head_dim):
            inv_freq = 1.0 / ROPE_BASE ** (jnp.arange(0, head_dim, 2, dtype=jnp.float32) / head_dim)
            pos = jnp.arange(seq_len, dtype=jnp.float32)
            freqs = pos[:, None] * inv_freq[None, :]
            emb = jnp.repeat(freqs, 2, axis=-1)
            return (jnp.cos(emb)[None, None], jnp.sin(emb)[None, None])
        B, S, D = x.shape
        H = N_HEADS
        hd = D // H
        scale = hd ** (-0.5)

        def shape_heads(t):
            return t.reshape(B, S, H, hd).transpose(0, 2, 1, 3)
        q = shape_heads(x @ Wq.T)
        k = shape_heads(x @ Wk.T)
        v = shape_heads(x @ Wv.T)
        cos, sin = _rope_cos_sin(S, hd)
        q = q * cos + _rotate_every_two(q) * sin
        k = k * cos + _rotate_every_two(k) * sin
        scores = jnp.einsum('bhqd,bhkd->bhqk', q, k) * scale
        qpos = jnp.arange(S)[:, None]
        kpos = jnp.arange(S)[None, :]
        mask = jnp.where(kpos > qpos, jnp.float32(-jnp.inf), jnp.float32(0.0))
        scores = scores + mask[None, None]
        attn = jax.nn.softmax(scores.astype(jnp.float32), axis=-1).astype(q.dtype)
        out = jnp.einsum('bhqk,bhkd->bhqd', attn, v)
        out = out.transpose(0, 2, 1, 3).reshape(B, S, D)
        return out @ Wo.T

    def _L0_ffn_ref(hidden_states, w_red, wg, W1, b1, W2, b2):
        import jax, jax.numpy as jnp
        import numpy as np
        B, T, E, C, H, G = (2, 512, 8, 256, 512, 16)
        b, t, c = hidden_states.shape
        x = hidden_states.reshape(-1, c)
        x_red = x @ w_red
        wg_n = wg / jnp.maximum(jnp.linalg.norm(wg, axis=1, keepdims=True), 0.0001)
        logits = x_red @ wg_n.T
        gates = jax.nn.softmax(logits, axis=1)
        scores = jnp.max(gates, axis=1)
        idx = jnp.argmax(gates, axis=1)
        h = jnp.einsum('nc,ech->neh', x, W1) + b1[None]
        h = jnp.take_along_axis(h, idx[:, None, None], axis=1)[:, 0, :]
        h = jax.nn.gelu(h, approximate=False)
        o = jnp.einsum('nh,ehc->nec', h, W2) + b2[None]
        o = jnp.take_along_axis(o, idx[:, None, None], axis=1)[:, 0, :]
        o = o * scores[:, None]
        return o.reshape(b, t, c)

    def _L1_attn_ref(x, qkv_w, qkv_b, rq_w, rq_b, rkv_w, rkv_b, rout_w, rout_b, out_w, out_b, gl_w, gr_w):
        import jax, jax.numpy as jnp
        import numpy as np
        D_MODEL = 256
        N_HEADS = 16
        HEAD_DIM = D_MODEL // N_HEADS
        WINDOW = 128
        LOCAL_BLOCK = 64
        LATENT_TOKENS = 64
        LATENT_D = 64
        LATENT_HEADS = 4
        LATENT_HD = LATENT_D // LATENT_HEADS
        NEG = -1000000000.0

        def _local_attention(q, k, v):
            B, H, S, hd = q.shape
            bs = min(S, max(WINDOW, LOCAL_BLOCK))
            nb = S // bs
            w = WINDOW
            L = bs + w - 1
            k_pad = jnp.pad(k, ((0, 0), (0, 0), (w - 1, 0), (0, 0)))
            v_pad = jnp.pad(v, ((0, 0), (0, 0), (w - 1, 0), (0, 0)))
            starts = jnp.arange(nb) * bs
            idx = starts[:, None] + jnp.arange(L)[None, :]
            kb = k_pad[:, :, idx]
            vb = v_pad[:, :, idx]
            qb = q.reshape(B, H, nb, bs, hd)
            q_pos = starts[:, None] + jnp.arange(bs)[None, :]
            k_gpos = starts[:, None] + jnp.arange(L)[None, :] - (w - 1)
            dist = q_pos[:, :, None] - k_gpos[:, None, :]
            allowed = (dist > 0) & (dist <= w) & (k_gpos[:, None, :] >= 0)
            scale = 1.0 / np.sqrt(hd)
            scores = jnp.einsum('bhnqd,bhnkd->bhnqk', qb, kb) * scale
            scores = jnp.where(allowed, scores, NEG)
            attn = jax.nn.softmax(scores, axis=-1)
            attn = jnp.where(allowed.any(-1)[None, None, :, :, None], attn, 0.0)
            out = jnp.einsum('bhnqk,bhnkd->bhnqd', attn, vb)
            return out.reshape(B, H, S, hd)
        B, S, D = x.shape
        qkv = x @ qkv_w + qkv_b
        q, k, v = jnp.split(qkv, 3, axis=-1)

        def heads(t):
            return t.reshape(B, S, N_HEADS, HEAD_DIM).transpose(0, 2, 1, 3)
        local = _local_attention(heads(q), heads(k), heads(v))
        chunk = -(-S // min(LATENT_TOKENS, S))
        nlat = S // chunk
        pooled = x.reshape(B, nlat, chunk, D).mean(axis=2)
        chunk_ids = jnp.arange(S) // chunk
        rq = (x @ rq_w + rq_b).reshape(B, S, LATENT_HEADS, LATENT_HD).transpose(0, 2, 1, 3)
        rkv = pooled @ rkv_w + rkv_b
        rk, rv = jnp.split(rkv, 2, axis=-1)
        rk = rk.reshape(B, nlat, LATENT_HEADS, LATENT_HD).transpose(0, 2, 1, 3)
        rv = rv.reshape(B, nlat, LATENT_HEADS, LATENT_HD).transpose(0, 2, 1, 3)
        lscale = 1.0 / np.sqrt(LATENT_HD)
        lscores = jnp.einsum('bhsd,bhld->bhsl', rq, rk) * lscale
        lat_allowed = jnp.arange(nlat)[None, :] < chunk_ids[:, None]
        lscores = jnp.where(lat_allowed[None, None], lscores, NEG)
        lattn = jax.nn.softmax(lscores, axis=-1)
        lattn = jnp.where(lat_allowed.any(-1)[None, None, :, None], lattn, 0.0)
        lat_out = jnp.einsum('bhsl,bhld->bhsd', lattn, rv)
        lat_out = lat_out.transpose(0, 2, 1, 3).reshape(B, S, LATENT_D)
        remote = lat_out @ rout_w + rout_b
        remote_h = remote.reshape(B, S, N_HEADS, HEAD_DIM).transpose(0, 2, 1, 3)
        gate = jax.nn.sigmoid(local @ gl_w + remote_h @ gr_w)
        mixed = gate * local + (1.0 - gate) * remote_h
        mixed = mixed.transpose(0, 2, 1, 3).reshape(B, S, D)
        return mixed @ out_w + out_b

    def _L1_ffn_ref(x, ln_g, ln_b, bn_g, bn_b, bn_mean, bn_var, Wr, br, W_down, b_down, W_up, b_up):
        import jax, jax.numpy as jnp
        import numpy as np
        B, S, D, H, E = (64, 256, 256, 64, 8)
        EPS = 1e-05
        mu = jnp.mean(x, axis=-1, keepdims=True)
        var = jnp.var(x, axis=-1, keepdims=True)
        z = (x - mu) * jax.lax.rsqrt(var + EPS) * ln_g + ln_b
        z_sent = jnp.mean(z, axis=1)
        z_bn = (z_sent - bn_mean) * jax.lax.rsqrt(bn_var + EPS) * bn_g + bn_b
        probs = jax.nn.softmax(z_bn @ Wr + br, axis=-1)
        idx = jnp.argmax(probs, axis=-1)
        gate = jnp.take_along_axis(probs, idx[:, None], axis=1)[:, 0]
        h = jax.nn.relu(jnp.einsum('bsd,bdh->bsh', z, W_down[idx]) + b_down[idx][:, None, :])
        y = jnp.einsum('bsh,bhd->bsd', h, W_up[idx]) + b_up[idx][:, None, :]
        return y * gate[:, None, None]
    x = L0_attn_x
    x = _layernorm(x + _L0_attn_ref(x, L0_attn_Wq, L0_attn_Wk, L0_attn_Wv, L0_attn_Wo), axis=-1)
    x = _layernorm(x + _L0_ffn_ref(x, L0_ffn_w_red, L0_ffn_wg, L0_ffn_W1, L0_ffn_b1, L0_ffn_W2, L0_ffn_b2), axis=-1)
    x = _layernorm(x + _L1_attn_ref(x, L1_attn_qkv_w, L1_attn_qkv_b, L1_attn_rq_w, L1_attn_rq_b, L1_attn_rkv_w, L1_attn_rkv_b, L1_attn_rout_w, L1_attn_rout_b, L1_attn_out_w, L1_attn_out_b, L1_attn_gl_w, L1_attn_gr_w), axis=-1)
    x = _layernorm(x + _L1_ffn_ref(x, L1_ffn_ln_g, L1_ffn_ln_b, L1_ffn_bn_g, L1_ffn_bn_b, L1_ffn_bn_mean, L1_ffn_bn_var, L1_ffn_Wr, L1_ffn_br, L1_ffn_W_down, L1_ffn_b_down, L1_ffn_W_up, L1_ffn_b_up), axis=-1)
    return x

_drawn_inputs = setup_inputs


def setup_inputs(seed=0):
    import zlib

    import numpy as np

    out = dict(_drawn_inputs(seed))
    spreads = {'L1_attn_qkv_b': (0.0, 0.466),
     'L1_attn_rq_b': (0.0, 0.8),
     'L1_attn_rkv_b': (0.0, 0.8),
     'L1_attn_rout_b': (0.0, 0.417),
     'L1_attn_out_b': (0.0, 0.1),
     'L1_ffn_ln_g': (1.0, 0.6),
     'L1_ffn_ln_b': (0.0, 0.512),
     'L1_ffn_bn_g': (1.0, 0.6),
     'L1_ffn_bn_b': (0.0, 0.505),
     'L1_ffn_bn_var': (1.0, 0.6),
     'L1_ffn_br': (0.0, 1.889),
     'L1_ffn_b_down': (0.0, 0.8),
     'L1_ffn_b_up': (0.0, 0.594)}
    factors = {'L0_attn_Wq': 8.0,
     'L0_attn_Wk': 8.0,
     'L0_attn_Wv': 4.661,
     'L0_attn_Wo': 4.33,
     'L0_ffn_w_red': 3.949,
     'L0_ffn_wg': 3.936,
     'L0_ffn_W1': 3.722,
     'L0_ffn_b1': 8.0,
     'L0_ffn_W2': 3.624,
     'L0_ffn_b2': 8.0,
     'L1_attn_qkv_w': 8.0,
     'L1_attn_rq_w': 8.0,
     'L1_attn_rkv_w': 8.0,
     'L1_attn_rout_w': 8.0,
     'L1_attn_gl_w': 8.0,
     'L1_attn_gr_w': 8.0,
     'L1_ffn_bn_mean': 41.37,
     'L1_ffn_Wr': 8.0,
     'L1_ffn_W_down': 8.0,
     'L1_ffn_W_up': 8.0}
    for name, (base, spread) in spreads.items():
        noise = np.random.default_rng([zlib.crc32(name.encode()), seed]).standard_normal(out[name].shape)
        drawn = base * np.exp(spread * noise) if base else spread * noise
        out[name] = jnp.asarray(drawn.astype(out[name].dtype))
    for name, factor in factors.items():
        out[name] = (out[name] * factor).astype(out[name].dtype)
    return out
```

```python
import concourse.bass as bass
from concourse import mybir
from contextlib import ExitStack

f32 = mybir.dt.float32
bf16 = mybir.dt.bfloat16
i32 = mybir.dt.int32
u32 = mybir.dt.uint32
ALU = mybir.AluOpType
ACT = mybir.ActivationFunctionType
AX = mybir.AxisListType

P = 128
B, S, D = 8, 512, 256
H, HD = 16, 16
NT = S // P
KC = D // P
TILES = B * NT
E, F = 8, 512
G0 = 16
MT = TILES + E - 1
MSTEP = 13
E1, F1 = 8, 64
LAT, CH = 64, S // 64
LH = 4
LD = LH * HD
NEG = -1e30
EPS = 1e-5
SCALE = HD ** -0.5
PARTS = 6
ROWS = PARTS * HD
KROWS = ROWS + 3
GH = 4
NG = H // GH
VW = 32
TW = H * ROWS + 2 * HD


class Loop:

    def __init__(self, nc, ctx, names):
        self.nc = nc
        self.sems = {n: ctx.enter_context(nc.semaphore(n)) for n in names}
        nums = sorted(s.num for s in self.sems.values())
        cuts = [i for i in range(1, len(nums)) if nums[i] != nums[i - 1] + 1]
        self.runs = [range(nums[a], nums[b - 1] + 1) for a, b in zip([0] + cuts, cuts + [len(nums)])]

    def __getitem__(self, name):
        return self.sems[name]

    def clear(self):
        for run in self.runs:
            self.nc.sync.sem_clear(run)
        self.nc.all_engine_barrier(sem_only=True)


class Chain:

    def __init__(self, eng, sem):
        self.eng, self.sem, self.n = eng, sem, 0

    def step(self, ins):
        ins.then_inc(self.sem, 1)
        self.n += 1

    def settle(self):
        self.eng.wait_ge(self.sem, self.n)


class Plan:

    def __init__(self, causal):
        self.causal = causal
        if causal:
            self.smax = [(3, [h]) for h in range(GH)] + [(2, [h]) for h in range(GH)]
            self.smax += [(1, [0, 1]), (1, [2, 3]), (0, [0, 1, 2, 3])]
        else:
            self.smax = [(q, hs) for q in (1, 2, 3) for hs in ([0, 1], [2, 3])] + [(0, [0, 1, 2, 3])]
        self.at = {0: 0, 1: 512, 3: 896, 2: 1024} if causal else {0: 0, 1: 256, 2: 512, 3: 768}
        self.width = 1280 if causal else 896
        self.sexp = [[(h, k, self.at[k]) for k in ((0, 1, 3) if causal else (0, 1, 2, 3))] for h in range(GH)]
        if causal:
            self.sexp.append([(h, 2, 256 * h) for h in range(GH)])

    def keys(self, q):
        first = 0 if self.causal else max(0, q - 1)
        return first * P, (q + 1) * P

    def queries(self, k):
        last = NT if self.causal else min(NT, k + 2)
        return k * P, last * P


def order(plan):
    def units(kind, g):
        n = len(plan.smax if kind == "max" else plan.sexp)
        return [(kind, g, u) for u in range(n)] + ([("split", g, 0)] if kind == "max" else [])

    seq = units("max", 0) + [("turn", 0, 0)] + units("max", 1)
    for g in range(NG):
        a = units("max", g + 2) if g + 2 < NG else []
        c = units("exp", g)
        each = -(-len(a) // len(c))
        part = []
        for n, u in enumerate(c):
            part += [u] + a[n * each:(n + 1) * each]
            if n == 0 and g >= 1:
                part.append(("values", g - 1, 0))
            if n == 0 and g + 1 < NG:
                part.append(("turn", g + 1, 0))
        seq += part
    return seq + [("values", NG - 1, 0)]


ATT = ["xt_in", "xt_ps", "xt_act", "xt_dve", "qk_ps", "qk_read", "qk_sum", "part1", "v_ps", "v_in", "rest1",
       "part2", "part3", "stack_ps", "stack_dve", "stack_act", "s_ps", "s_max", "m_split", "m_ps", "m_act",
       "m_dma0", "m_dma1", "m_dma2", "m_dma3", "c_ps", "exps", "pv_ps", "o_in", "d1_ps", "a_norm", "a_ps",
       "at_act", "at_dve", "y_ps", "y_in", "var", "rstd", "x_new", "kept", "act_chain", "dve_chain", "pool_chain"]


class Attention:

    def __init__(self, nc, ctx, plan, m, lp, bufs):
        self.nc, self.plan, self.m, self.lp, self.seq = nc, plan, m, lp, order(plan)
        self.QS, self.KS, self.PT, self.V, self.T = (bufs[k] for k in ("QS", "KS", "PT", "V", "T"))
        self.qk, self.rest, self.xT, self.OT, self.A = (bufs[k] for k in ("qk", "rest", "xT", "OT", "A"))
        self.nm, self.MB, self.MS, self.den, self.rec = (bufs[k] for k in ("nm", "MB", "MS", "den", "rec"))
        self.xb, self.y, self.xn, self.mv, self.st = (bufs[k] for k in ("xb", "y", "xn", "mv", "st"))
        self.ve, self.rstd = bufs["ve"], bufs["rstd"]

    def qk_summed(self, eng, n):
        eng.wait_ge(self.lp["qk_sum" if self.plan.causal else "qk_read"], n)

    def pe_turn_x(self, pe, src):
        m, lp = self.m, self.lp
        for c in range(KC):
            for t in range(NT):
                last = pe.transpose(m["ps"][c][:, t * P:(t + 1) * P], src[:, t, c * P:(c + 1) * P], m["idf"][:, :])
            last.then_inc(lp["xt_ps"], 1)

    def pe_project(self, pe, t, w):
        m, lp = self.m, self.lp
        if t >= 2:
            pe.wait_ge(lp["qk_read"], t - 1)
            pe.wait_ge(lp["v_in"], t - 1)
        pair = m["pair"][t % 2]
        for lo, hi, name in ((0, 2 * D, "qk_ps"), (2 * D, 3 * D, "v_ps")):
            for c in range(KC):
                last = pe.matmul(pair[:, lo:hi], self.xT[:, c, t * P:(t + 1) * P], w[:, c, lo:hi],
                                 start=(c == 0), stop=(c == KC - 1))
            last.then_inc(lp[name], 1)

    def pe_stack(self, pe, t):
        m, lp = self.m, self.lp
        pe.wait_ge(lp["part3"], 2 * t + 2)
        for i in range(4):
            if t >= 1:
                pe.wait_ge(lp["stack_act" if i % 2 else "stack_dve"], 2 * (t - 1) + i // 2 + 1)
            bank = m["ps"][i]
            for n in range(8):
                h = (i % 2) * 8 + n
                off = h * ROWS + (0 if i >= 2 else 2 * HD)
                last = pe.transpose(bank[0:ROWS, n * 64:(n + 1) * 64].bitcast(bf16),
                                    self.T[t % 2][:, i // 2, off:off + ROWS], m["idb"][:, :])
            last.then_inc(lp["stack_ps"], 1)

    def pe_tiles(self, pe, w):
        for s in range(NT + 2):
            if s < NT:
                self.pe_project(pe, s, w)
            if s >= 2:
                self.pe_stack(pe, s - 2)

    def pe_attend(self, pe):
        m, lp, plan = self.m, self.lp, self.plan
        mS, mT = (m["mS0"], m["mT0"]) if plan.causal else (m["mS1"], m["mT1"])
        pe.wait_ge(lp["stack_dve"], 2 * NT)
        pe.wait_ge(lp["stack_act"], 2 * NT)
        pe.wait_ge(lp["qk_read"], NT)
        pe.wait_ge(lp["v_in"], NT)
        for kind, g, u in self.seq:
            if kind == "max":
                n = g * len(plan.smax) + u
                if n >= 2:
                    pe.wait_ge(lp["s_max"], n - 1)
                qt, heads = plan.smax[u]
                k0, k1 = plan.keys(qt)
                w = k1 - k0
                for i, hh in enumerate(heads):
                    o = m["ps"][n % 2][:, i * w:(i + 1) * w]
                    h = g * GH + hh
                    pe.matmul(o, self.QS[0:ROWS, h, qt * P:(qt + 1) * P], self.KS[0:ROWS, h, k0:k1],
                              start=True, stop=True)
                    if plan.causal:
                        o, mask = o[:, w - P:w], mS[:, :]
                    else:
                        mask = mS[:, 2 * P - w:2 * P]
                    last = pe.matmul(o, m["idb"][:, :], mask, start=False, stop=True, skip_group_check=True)
                last.then_inc(lp["s_ps"], 1)
            elif kind == "turn":
                pe.wait_ge(lp["m_split"], g + 1)
                if g >= 1:
                    pe.wait_ge(lp["m_act"], g)
                for t in range(NT):
                    last = pe.transpose(m["ps"][3][0:3 * GH, t * 64:(t + 1) * 64].bitcast(bf16),
                                        self.MB[:, g, t, :], m["idb"][:, :])
                last.then_inc(lp["m_ps"], 1)
            elif kind == "exp":
                n = g * len(plan.sexp) + u
                if u == 0:
                    pe.wait_ge(lp[f"m_dma{g}"], 48)
                if n >= 2:
                    pe.wait_ge(lp["exps"], n - 1)
                for hh, kt, off in plan.sexp[u]:
                    q0, q1 = plan.queries(kt)
                    w = q1 - q0
                    h = g * GH + hh
                    o = m["pair"][n % 2][:, off:off + w]
                    pe.matmul(o, self.KS[0:KROWS, h, kt * P:(kt + 1) * P], self.QS[0:KROWS, h, q0:q1],
                              start=True, stop=True)
                    if plan.causal:
                        o, mask = o[:, 0:P], mT[:, :]
                    else:
                        mask = mT[:, 0:w]
                    last = pe.matmul(o, m["idb"][:, :], mask, start=False, stop=True, skip_group_check=True)
                last.then_inc(lp["c_ps"], 1)
            elif kind == "values":
                pe.wait_ge(lp["exps"], len(plan.sexp) * (g + 1))
                if g >= 1:
                    pe.wait_ge(lp["o_in"], g)
                for kt in range(NT):
                    q0, q1 = plan.queries(kt)
                    off = plan.at[kt]
                    for hh in range(GH):
                        last = pe.matmul(m["ps"][2][VW * hh:VW * (hh + 1), q0:q1],
                                         self.V[:, kt, g * GH + hh, :],
                                         self.PT[:, g % 2, hh, off:off + q1 - q0],
                                         start=(kt == 0), stop=True, skip_group_check=True)
                last.then_inc(lp["pv_ps"], 1)

    def pe_turn_o(self, pe):
        m, lp = self.m, self.lp
        pe.wait_ge(lp["o_in"], NG)
        pe.wait_ge(lp["s_max"], NG * len(self.plan.smax))
        for t in range(NT):
            if t >= 2:
                pe.wait_ge(lp["a_norm"], t - 1)
            for g in range(NG):
                last = pe.transpose(m["ps"][t % 2][:, g * P:(g + 1) * P], self.OT[:, g, t * P:(t + 1) * P],
                                    m["idf"][:, :])
            last.then_inc(lp["d1_ps"], 1)

    def pe_out(self, pe, src, w):
        m, lp = self.m, self.lp
        for c in range(KC):
            for t in range(NT):
                last = pe.transpose(m["pair"][0][:, c * S + t * P:c * S + (t + 1) * P],
                                    src[:, t, c * P:(c + 1) * P], m["idf"][:, :])
            last.then_inc(lp["a_ps"], 1)
        pe.wait_ge(lp["at_act"], 1)
        pe.wait_ge(lp["at_dve"], 1)
        for i in range(2):
            for t in (2 * i, 2 * i + 1):
                o = m["pair"][1][:, t * D:(t + 1) * D]
                for c in range(KC):
                    last = pe.matmul(o, self.xT[:, c, t * P:(t + 1) * P], w[:, c, :],
                                     start=(c == 0), stop=(c == KC - 1))
            last.then_inc(lp["y_ps"], 1)

    def act_tile(self, act, t):
        lp = self.lp
        self.qk_summed(act, t + 1)
        if t >= 2:
            act.wait_ge(lp["stack_ps"], 4 * (t - 1))
        first = self.T[t % 2][:, :, 2 * HD:].rearrange("p a (h s) -> p a h s", s=ROWS)[:, :, :, 0:3 * HD]
        src = self.qk[:, t % 2, :].rearrange("p (h r c) -> p h r c", r=1, c=HD).to_broadcast([P, 2 * H, 3, HD])
        act.activation(first, src, ACT.Copy).then_inc(lp["part1"], 1)

    def act_stacks(self, act, t):
        m, lp = self.m, self.lp
        for i in (1, 3):
            act.wait_ge(lp["stack_ps"], 4 * t + i + 1)
            dst = (self.QS, self.KS)[i // 2][0:ROWS, 8:16, t * P:(t + 1) * P]
            act.activation(dst, m["ps"][i][0:ROWS, :].bitcast(bf16).rearrange("p (h q) -> p h q", h=8), ACT.Copy)\
               .then_inc(lp["stack_act"], 1)

    def act_attend(self, act):
        m, lp, plan = self.m, self.lp, self.plan
        for kind, g, u in self.seq:
            if kind == "turn":
                act.wait_ge(lp["m_ps"], g + 1)
                act.activation(self.MS[:, g, :], m["ps"][3][0:3 * GH, 0:S // 2].bitcast(bf16), ACT.Copy)\
                   .then_inc(lp["m_act"], 1)
            elif kind == "exp":
                n = g * len(plan.sexp) + u
                act.wait_ge(lp["c_ps"], n + 1)
                if g >= 2 and u == 0:
                    act.wait_ge(lp["pv_ps"], g - 1)
                pair = m["pair"][n % 2]
                if u < GH:
                    w = min(plan.width, 1024)
                    o, i = self.PT[:, g % 2, u, 0:w], pair[:, 0:w]
                else:
                    o, i = self.PT[:, g % 2, :, 1024:1280], pair[:, :].rearrange("p (h q) -> p h q", h=GH)
                act.activation(o, i, ACT.Exp, scale=SCALE).then_inc(lp["exps"], 1)

    def dve_rest1(self, dve, t):
        lp = self.lp
        dve.wait_ge(lp["part1"], t + 1)
        if t >= 1:
            dve.wait_ge(lp["part2"], 3 * t)
            dve.wait_ge(lp["part3"], 2 * t)
        first = self.T[t % 2][:, :, 2 * HD:].rearrange("p a (h s) -> p a h s", s=ROWS)[:, :, :, 0:HD]
        dve.tensor_tensor(self.rest[:, :].rearrange("p (a h c) -> p a h c", a=2, c=HD),
                          self.qk[:, t % 2, :].rearrange("p (a h c) -> p a h c", a=2, c=HD),
                          first, ALU.subtract).then_inc(lp["rest1"], 1)

    def half(self, t, a, slot):
        lo = (2 * HD if a == 0 else 0)
        return self.T[t % 2][:, a, lo:lo + H * ROWS].rearrange("p (h s) -> p h s", s=ROWS)[:, :, slot * HD:(slot + 1) * HD]

    def rest_of(self, a):
        return self.rest[:, a * D:(a + 1) * D].rearrange("p (h c) -> p h c", c=HD)

    def dve_part3(self, dve, t):
        lp = self.lp
        dve.wait_ge(lp["part2"], 3 * t + 3)
        for a, slot2, slot3 in ((0, 3, 4), (1, 5, 1)):
            dve.tensor_tensor(self.half(t, a, slot3), self.rest_of(a), self.half(t, a, slot2), ALU.subtract)\
               .then_inc(lp["part3"], 1)

    def dve_stacks(self, dve, t):
        m, lp = self.m, self.lp
        for i in (0, 2):
            dve.wait_ge(lp["stack_ps"], 4 * t + i + 1)
            dst = (self.QS, self.KS)[i // 2][0:ROWS, 0:8, t * P:(t + 1) * P].bitcast(i32)
            dve.tensor_copy(dst, m["ps"][i][0:ROWS, :].bitcast(i32).rearrange("p (h w) -> p h w", h=8))\
               .then_inc(lp["stack_dve"], 1)

    def dve_attend(self, dve, ch):
        m, lp, plan = self.m, self.lp, self.plan
        for kind, g, u in self.seq:
            if kind == "max":
                n = g * len(plan.smax) + u
                dve.wait_ge(lp["s_ps"], n + 1)
                qt, heads = plan.smax[u]
                k0, k1 = plan.keys(qt)
                w = (k1 - k0) * len(heads)
                dve.tensor_reduce(self.nm[:, g, qt, heads[0]:heads[0] + len(heads)],
                                  m["ps"][n % 2][:, 0:w].rearrange("p (h k) -> p h k", h=len(heads)),
                                  AX.X, ALU.max, negate=True).then_inc(lp["s_max"], 1)
            elif kind == "split":
                dve.wait_ge(lp["s_max"], (g + 1) * len(plan.smax))
                nm, MB = self.nm[:, g, :, :], self.MB[:, g, :, :]
                if not plan.causal:
                    ch.step(dve.tensor_scalar(nm, nm, -NEG / 10, None, ALU.min))
                    ch.settle()
                for r in range(3):
                    part = MB[:, :, r * GH:(r + 1) * GH]
                    if r < 2:
                        ch.step(dve.tensor_copy(part, nm))
                        ch.settle()
                        ch.step(dve.tensor_tensor(nm, nm, part, ALU.subtract))
                        ch.settle()
                    else:
                        dve.tensor_copy(part, nm).then_inc(lp["m_split"], 1)
            elif kind == "values":
                dve.wait_ge(lp["pv_ps"], g + 1)
                dve.tensor_copy(self.OT[:, g, :], m["ps"][2][:, :]).then_inc(lp["o_in"], 1)

    def dve_normalise(self, dve, ch):
        m, lp = self.m, self.lp
        for t in range(NT):
            dve.wait_ge(lp["d1_ps"], t + 1)
            o = m["ps"][t % 2][:, :].rearrange("p (h c) -> p h c", c=VW)
            den, rec = self.den[:, t, :], self.rec[:, t, :]
            if self.plan.causal:
                ch.step(dve.reciprocal(rec, o[:, :, HD]))
            else:
                ch.step(dve.tensor_scalar(den, o[:, :, HD], -1.0 / NEG, None, ALU.max))
                ch.settle()
                ch.step(dve.reciprocal(rec, den))
            ch.settle()
            dve.tensor_tensor(self.A[:, t, :].rearrange("p (h c) -> p h c", c=HD), o[:, :, 0:HD],
                              rec.rearrange("p (h c) -> p h c", c=1).to_broadcast([P, H, HD]), ALU.mult)\
               .then_inc(lp["a_norm"], 1)

    def pool_part2(self, pool, t):
        lp = self.lp
        pool.wait_ge(lp["rest1"], t + 1)
        both = self.T[t % 2][:, :, 2 * HD:].rearrange("p a (h s) -> p a h s", s=ROWS)[:, :, :, 3 * HD:4 * HD]
        pool.tensor_scalar(both, self.rest[:, :].rearrange("p (a h c) -> p a h c", a=2, c=HD), 1.0, 0.0,
                           ALU.mult, ALU.add).then_inc(lp["part2"], 1)
        pool.tensor_scalar(self.half(t, 0, 5), self.rest_of(0), 1.0, 0.0, ALU.mult, ALU.add).then_inc(lp["part2"], 1)
        pool.tensor_scalar(self.half(t, 1, 0), self.rest_of(1), 1.0, 0.0, ALU.mult, ALU.add).then_inc(lp["part2"], 1)

    def sp_maxima(self, sp):
        lp = self.lp
        for g in range(NG):
            sp.wait_ge(lp["m_act"], g + 1)
            for r in range(3):
                sp.dma_start(self.QS[ROWS + r:ROWS + r + 1, g * GH:(g + 1) * GH, :], self.MS[r * GH:(r + 1) * GH, g, :])\
                  .then_inc(lp[f"m_dma{g}"], 16)


def dve_layernorm(dve, lp, ch, y, mv, st, ve, rstd, out, turn):
    for t in range(NT):
        ch.step(dve.bn_stats(st[:, t, :], y[:, t, :]))
    ch.settle()
    for t in range(NT):
        ch.step(dve.bn_aggr(mv[:, t, :], st[:, t, :]))
    ch.settle()
    dve.tensor_scalar(ve, mv[:, :, 1], EPS, None, ALU.add).then_inc(lp["var"], 1)
    dve.wait_ge(lp["rstd"], turn)
    for t in range(NT):
        dve.tensor_scalar(out[:, t, :], y[:, t, :], mv[:, t, 0:1], rstd[:, t:t + 1], ALU.subtract, ALU.mult)\
           .then_inc(lp["x_new"], 1)


def pool_rstd(pool, lp, ve, rstd, half, turn):
    pool.wait_ge(lp["var"], turn)
    pool.tensor_tensor(rstd, ve, half, ALU.pow).then_inc(lp["rstd"], 1)


def attention_buffers(nc, ctx, tag, plan):
    def sb(name, shape, dt=f32):
        return ctx.enter_context(nc.sbuf_tensor(f"{name}{tag}", shape, dt))

    both, attended = sb("parts", [P, 2 * TW]), sb("attended", [P, NT, D])
    return {
        "QS": sb("q_stack", [P, H, S], bf16), "KS": sb("k_stack", [P, H, S], bf16),
        "PT": sb("probs", [P, 2, GH, plan.width]), "V": sb("values", [P, NT, H, VW]),
        "T": [both[:, i * TW:(i + 1) * TW].bitcast(bf16).rearrange("p (a w) -> p a w", a=2) for i in range(2)],
        "qk": sb("qk", [P, 2, 2 * D]), "rest": sb("rest", [P, 2 * D]), "xT": sb("xT", [P, KC, S]),
        "OT": both[:, 0:NG * S].rearrange("p (g s) -> p g s", g=NG), "A": attended, "nm": sb("maxima", [P, NG, NT, GH]),
        "MB": sb("m_parts", [P, NG, NT, 3 * GH], bf16), "MS": both[0:3 * GH, NG * S:NG * S + NG * S // 2].bitcast(bf16).rearrange("p (g s) -> p g s", g=NG),
        "den": sb("sums", [P, NT, H]), "rec": sb("recips", [P, NT, H]),
        "xb": sb("x_batch", [P, NT, D]), "y": sb("y", [P, NT, D]), "xn": attended,
        "mv": sb("mean_var", [P, NT, 2]), "st": sb("stats", [P, NT, 6]), "ve": sb("var_eps", [P, NT]),
        "rstd": sb("rstd", [P, NT]),
    }


def start_buffers(dve, bufs, sem):
    dve.memset(bufs["V"][:, :, :, :], 0.0).then_inc(sem, 1)
    dve.memset(bufs["KS"][ROWS:KROWS, :, :], 1.0).then_inc(sem, 1)
    dve.wait_ge(sem, 1)
    dve.memset(bufs["V"][:, :, :, HD:HD + 1], 1.0).then_inc(sem, 1)


def spread(ap, n, count):
    return ap.rearrange("p (r c) -> p r c", r=1).to_broadcast([P, count, n])


CONST = {"id": P, "mS0": P, "mT0": P, "mS1": 2 * P, "mT1": 2 * P, "tri": P, "cos": NT * HD, "sin": NT * HD,
         "lat": NT * LAT, "heads": LH, "less": E}
CASTS = 8 * P


def layer0_attention(nc, m, g, w):
    plan = Plan(causal=True)
    with ExitStack() as ctx:
        bufs = attention_buffers(nc, ctx, "0", plan)
        halves = ctx.enter_context(nc.sbuf_tensor("rope_halves", [P, 2, 2, 2 * D], f32))
        xrT = ctx.enter_context(nc.sbuf_tensor("x_reduced", [G0, S], f32))
        ready = ctx.enter_context(nc.semaphore("buffers0"))
        lp = Loop(nc, ctx, ATT + ["rt_ps", "rt_act", "rt_dve", "xr_ps", "xr_in", "lg_ps"])
        at = Attention(nc, ctx, plan, m, lp, bufs)
        x_all, xb, y, xn, xT = g["x_all"], at.xb, at.y, at.xn, at.xT

        with nc.Block() as block:
            @block.vector
            def _(dve):
                start_buffers(dve, bufs, ready)

        with nc.Fori(0, B) as b:
            with nc.Block(no_gpsimd_drain=True) as block:
                @block.sync
                def _(sp):
                    at.sp_maxima(sp)

                @block.tensor
                def _(pe):
                    pe.wait_ge(lp["xt_in"], 1)
                    at.pe_turn_x(pe, xb)
                    pe.wait_ge(lp["xt_act"], 1)
                    pe.wait_ge(lp["xt_dve"], 1)
                    at.pe_tiles(pe, w["qkv0"])
                    at.pe_attend(pe)
                    at.pe_turn_o(pe)
                    pe.wait_ge(lp["a_norm"], NT)
                    at.pe_out(pe, at.A, w["o0"])
                    pe.wait_ge(lp["x_new"], NT)
                    pe.wait_ge(lp["m_act"], NG)
                    for c in range(KC):
                        for t in range(NT):
                            last = pe.transpose(m["ps"][2 + c][:, t * P:(t + 1) * P], xn[:, t, c * P:(c + 1) * P],
                                                m["idf"][:, :])
                        last.then_inc(lp["rt_ps"], 1)
                    pe.wait_ge(lp["rt_act"], 1)
                    pe.wait_ge(lp["rt_dve"], 1)
                    for c in range(KC):
                        last = pe.matmul(m["ps"][0][0:G0, :], w["red"][:, c, :], xT[:, c, :],
                                         start=(c == 0), stop=(c == KC - 1))
                    last.then_inc(lp["xr_ps"], 1)
                    pe.wait_ge(lp["xr_in"], 1)
                    for t in range(NT):
                        last = pe.matmul(m["ps"][1][:, t * E:(t + 1) * E], xrT[:, t * P:(t + 1) * P],
                                         w["gT"][:, :], start=True, stop=True)
                    last.then_inc(lp["lg_ps"], 1)

                @block.scalar
                def _(act):
                    act.wait_ge(lp["xt_ps"], 1)
                    act.activation(xT[:, 0, :], m["ps"][0][:, :], ACT.Copy).then_inc(lp["xt_act"], 1)
                    for s in range(NT + 2):
                        if s < NT:
                            at.act_tile(act, s)
                            act.wait_ge(lp["v_ps"], s + 1)
                            act.activation(at.V[:, s, :, 0:HD],
                                           m["pair"][s % 2][:, 2 * D:3 * D].rearrange("p (h c) -> p h c", c=HD),
                                           ACT.Copy).then_inc(lp["v_in"], 1)
                        if s >= 2:
                            at.act_stacks(act, s - 2)
                    at.act_attend(act)
                    act.wait_ge(lp["a_ps"], 1)
                    act.activation(xT[:, 0, :], m["pair"][0][:, 0:S], ACT.Copy).then_inc(lp["at_act"], 1)
                    act.wait_ge(lp["rt_ps"], 1)
                    act.wait_ge(lp["y_ps"], 2)
                    act.activation(xT[:, 0, :], m["ps"][2][:, :], ACT.Copy).then_inc(lp["rt_act"], 1)
                    act.wait_ge(lp["xr_ps"], 1)
                    act.activation(xrT[:, :], m["ps"][0][0:G0, :], ACT.Copy).then_inc(lp["xr_in"], 1)

                @block.vector
                def _(dve):
                    ch = Chain(dve, lp["dve_chain"])
                    dve.tensor_copy(xb[:, :, :], x_all[:, bass.ts(b, NT), :]).then_inc(lp["xt_in"], 1)
                    dve.wait_ge(lp["xt_ps"], 2)
                    dve.tensor_copy(xT[:, 1, :], m["ps"][1][:, :]).then_inc(lp["xt_dve"], 1)
                    for s in range(NT + 3):
                        if s < NT:
                            dve.wait_ge(lp["qk_ps"], s + 1)
                            if s >= 2:
                                dve.wait_ge(lp["qk_sum"], s - 1)
                            o = m["pair"][s % 2][:, 0:2 * D]
                            cos = m["cos"][:, s * HD:(s + 1) * HD]
                            sin = m["sin"][:, s * HD:(s + 1) * HD]
                            ch.step(dve.tensor_tensor(
                                halves[:, s % 2, 0, :].rearrange("p (h c) -> p h c", c=HD),
                                o.rearrange("p (h c) -> p h c", c=HD), spread(cos, HD, 2 * H), ALU.mult))
                            dve.tensor_tensor(
                                halves[:, s % 2, 1, :].rearrange("p (h c two) -> p h c two", two=2, c=HD // 2),
                                o.rearrange("p (h c two) -> p h c two", two=2, c=HD // 2)[:, :, :, ::-1],
                                sin.rearrange("p (r c two) -> p r c two", r=1, two=2)
                                   .to_broadcast([P, 2 * H, HD // 2, 2]), ALU.mult).then_inc(lp["qk_read"], 1)
                        if 2 <= s < NT + 2:
                            at.dve_part3(dve, s - 2)
                        if 1 <= s < NT + 1:
                            at.dve_rest1(dve, s - 1)
                        if s >= 3:
                            at.dve_stacks(dve, s - 3)
                    at.dve_attend(dve, ch)
                    at.dve_normalise(dve, ch)
                    dve.wait_ge(lp["a_ps"], 2)
                    dve.tensor_copy(xT[:, 1, :], m["pair"][0][:, S:2 * S]).then_inc(lp["at_dve"], 1)
                    for i in range(2):
                        dve.wait_ge(lp["y_ps"], i + 1)
                        dve.tensor_tensor(y[:, 2 * i:2 * i + 2, :], m["pair"][1][:, i * S:(i + 1) * S]
                                          .rearrange("p (t c) -> p t c", c=D), xb[:, 2 * i:2 * i + 2, :],
                                          ALU.add).then_inc(lp["y_in"], 1)
                    dve.wait_ge(lp["y_in"], 2)
                    dve_layernorm(dve, lp, ch, y, at.mv, at.st, at.ve[:, :], at.rstd, xn, 1)
                    dve.wait_ge(lp["x_new"], NT)
                    dve.tensor_copy(x_all[:, bass.ts(b, NT), :], xn[:, :, :])
                    dve.wait_ge(lp["rt_ps"], 2)
                    dve.tensor_copy(xT[:, 1, :], m["ps"][3][:, :]).then_inc(lp["rt_dve"], 1)
                    dve.wait_ge(lp["lg_ps"], 1)
                    dve.tensor_copy(g["logits"][:, bass.ts(b, NT), :],
                                    m["ps"][1][:, 0:NT * E].rearrange("p (t e) -> p t e", e=E))

                @block.gpsimd
                def _(pool):
                    for s in range(NT + 1):
                        if s < NT:
                            pool.wait_ge(lp["qk_read"], s + 1)
                            if s >= 2:
                                pool.wait_ge(lp["part1"], s - 1)
                                pool.wait_ge(lp["rest1"], s - 1)
                            pool.tensor_tensor(at.qk[:, s % 2, :], halves[:, s % 2, 0, :], halves[:, s % 2, 1, :],
                                               ALU.add).then_inc(lp["qk_sum"], 1)
                        if s >= 1:
                            at.pool_part2(pool, s - 1)
                    pool_rstd(pool, lp, at.ve[:, :], at.rstd[:, :], m["half"][:, :], 1)
            lp.clear()


def route(nc, m, g, xs_dram):
    with ExitStack() as ctx:
        def sb(name, shape, dt=f32):
            return ctx.enter_context(nc.sbuf_tensor(name, shape, dt))

        TE = TILES * E
        low = sb("neg_max", [P, TILES])
        lm = sb("logits_less_max", [P, TILES, E])
        ex = sb("exp_logits", [P, TILES, E])
        tot = sb("exp_sums", [P, TILES])
        sel = sb("is_max", [P, TILES, E])
        one = sb("one_hot", [P, TILES, E])
        oneb = sb("one_hot_bf", [P, TILES, E], bf16)
        which = sb("which", [P, TILES])
        rank = sb("rank", [P, TILES, E])
        count = sb("count", [P, TILES, E])
        run = [sb(f"running{i}", [P, TILES, E]) for i in range(2)]
        tiles_i = sb("tiles_i", [P, E], i32)
        tiles_f = sb("tiles_f", [P, E])
        ends = [sb(f"ends{i}", [P, E]) for i in range(2)]
        placef = sb("place_f", [P, TILES])
        past = sb("past", [P, MT + 1, E])
        onesb = sb("ones_bf", [P, P], bf16)
        sems = Loop(nc, ctx, ["dve_chain", "low", "exp", "hot", "ranked", "placed"])
        scattered = ctx.enter_context(nc.semaphore("scattered"))
        ps = m["ps"]
        with nc.Block() as block:
            @block.scalar
            def _(act):
                act.wait_ge(sems["low"], 1)
                act.activation(ex[:, :, :], lm[:, :, :], ACT.Exp).then_inc(sems["exp"], 1)

            @block.tensor
            def _(pe):
                pe.wait_ge(sems["hot"], 1)
                flat = oneb[:, :, :].rearrange("p t e -> p (t e)")
                pe.matmul(ps[0][:, 0:TE], m["tri"][:, :], flat, start=True, stop=True).then_inc(sems["ranked"], 1)
                pe.matmul(ps[1][:, 0:TE], onesb[:, :], flat, start=True, stop=True).then_inc(sems["ranked"], 1)

            @block.vector
            def _(dve):
                ch = Chain(dve, sems["dve_chain"])

                def step(ins):
                    ch.step(ins)
                    ch.settle()

                step(dve.memset(onesb[:, :], 1.0))
                step(dve.tensor_reduce(low[:, :], g["logits"][:, :, :], AX.X, ALU.max, negate=True))
                dve.tensor_tensor(lm[:, :, :], g["logits"][:, :, :],
                                  low[:, :].rearrange("p (t e) -> p t e", e=1).to_broadcast([P, TILES, E]),
                                  ALU.add).then_inc(sems["low"], 1)
                dve.wait_ge(sems["low"], 1)
                step(dve.tensor_scalar(sel[:, :, :], lm[:, :, :], 0.0, None, ALU.is_equal))
                less = m["less"][:, :].rearrange("p (r e) -> p r e", r=1).to_broadcast([P, TILES, E])
                step(dve.tensor_tensor(sel[:, :, :], sel[:, :, :], less, ALU.mult))
                step(dve.tensor_reduce(which[:, :], sel[:, :, :], AX.X, ALU.min))
                step(dve.tensor_tensor(one[:, :, :],
                                       which[:, :].rearrange("p (t e) -> p t e", e=1).to_broadcast([P, TILES, E]),
                                       less, ALU.is_equal))
                dve.tensor_copy(oneb[:, :, :], one[:, :, :]).then_inc(sems["hot"], 1)
                dve.wait_ge(sems["exp"], 1)
                step(dve.tensor_reduce(tot[:, :], ex[:, :, :], AX.X, ALU.add))
                step(dve.reciprocal(g["score"][:, :], tot[:, :]))
                dve.wait_ge(sems["ranked"], 2)
                step(dve.tensor_copy(rank[:, :, :], ps[0][:, 0:TE].rearrange("p (t e) -> p t e", e=E)))
                step(dve.tensor_copy(count[:, :, :], ps[1][:, 0:TE].rearrange("p (t e) -> p t e", e=E)))
                step(dve.tensor_copy(run[0][:, :, :], count[:, :, :]))
                cur, d = 0, 1
                while d < TILES:
                    a, z = run[cur], run[1 - cur]
                    step(dve.tensor_copy(z[:, 0:d, :], a[:, 0:d, :]))
                    step(dve.tensor_tensor(z[:, d:, :], a[:, d:, :], a[:, :TILES - d, :], ALU.add))
                    cur, d = 1 - cur, 2 * d
                total = run[cur][:, TILES - 1, :]
                step(dve.tensor_scalar(tiles_i[:, :], total, float(P - 1), None, ALU.add))
                step(dve.tensor_scalar(tiles_i[:, :], tiles_i[:, :], P.bit_length() - 1, None, ALU.arith_shift_right))
                step(dve.tensor_copy(tiles_f[:, :], tiles_i[:, :]))
                step(dve.tensor_copy(ends[0][:, :], tiles_f[:, :]))
                ce, d = 0, 1
                while d < E:
                    a, z = ends[ce], ends[1 - ce]
                    step(dve.tensor_copy(z[:, 0:d], a[:, 0:d]))
                    step(dve.tensor_tensor(z[:, d:], a[:, d:], a[:, :E - d], ALU.add))
                    ce, d = 1 - ce, 2 * d
                end = ends[ce]
                step(dve.tensor_tensor(tiles_f[:, :], end[:, :], tiles_f[:, :], ALU.subtract))
                step(dve.tensor_scalar(tiles_f[:, :], tiles_f[:, :], float(P), None, ALU.mult))
                step(dve.tensor_tensor(rank[:, :, :], rank[:, :, :], run[cur][:, :, :], ALU.add))
                step(dve.tensor_tensor(rank[:, :, :], rank[:, :, :], count[:, :, :], ALU.subtract))
                step(dve.tensor_tensor(rank[:, :, :], rank[:, :, :],
                                       tiles_f[:, :].rearrange("p (r e) -> p r e", r=1).to_broadcast([P, TILES, E]),
                                       ALU.add))
                step(dve.tensor_tensor(rank[:, :, :], rank[:, :, :], one[:, :, :], ALU.mult))
                step(dve.tensor_reduce(placef[:, :], rank[:, :, :], AX.X, ALU.add))
                dve.tensor_copy(g["place"][:, 0:TILES], placef[:, :]).then_inc(sems["placed"], 1)
                step(dve.memset(past[:, :, :], 0.0))
                for j in range(MT):
                    ins = dve.tensor_scalar(past[:, j, :], end[:, :], float(j), None, ALU.is_le)
                    ch.step(ins)
                ch.settle()
                step(dve.tensor_reduce(placef[:, 0:TILES], past[:, 0:TILES, :], AX.X, ALU.add))
                step(dve.tensor_scalar(g["expert"][:, 0:TILES], placef[:, :], float(E - 1), None, ALU.min))
                step(dve.tensor_reduce(placef[:, 0:MT + 1 - TILES], past[:, TILES:, :], AX.X, ALU.add))
                step(dve.tensor_scalar(g["expert"][:, TILES:MT + 1], placef[:, 0:MT + 1 - TILES], float(E - 1), None,
                                       ALU.min))
                step(dve.memset(g["place"][:, TILES:TILES + NT], 0))

            @block.gpsimd
            def _(pool):
                pool.wait_ge(sems["placed"], 1)
                for t in range(TILES):
                    pool.indirect_dma_start(xs_dram, bass.IndirectOffsetOnAxis(ap=g["place"][:, t:t + 1], axis=0),
                                            g["x_all"][:, t, :], None).then_inc(scattered, 16)
                pool.wait_ge(scattered, 16 * TILES)
        sems.clear()


def experts(nc, m, g, w_dram, xs_dram, ys_dram):
    NX = 3
    with ExitStack() as ctx:
        def sb(name, shape, dt=f32):
            return ctx.enter_context(nc.sbuf_tensor(name, shape, dt))

        FC = F // P
        W1 = sb("W1", [P, KC, E * F])
        W2 = sb("W2", [P, FC, E * D])
        b1 = sb("b1", [P, E * F])
        b2 = sb("b2", [P, E * D])
        xs = sb("xs", [P, NX, D])
        xsT = sb("xsT", [P, 2, KC * P])
        h = sb("h", [P, 2, F])
        hg = sb("h_gelu", [P, 2, F])
        hT = sb("hT", [P, 2, FC * P])
        ys = sb("ys", [P, 2, D])
        load = ctx.enter_context(nc.semaphore("expert_weights"))
        lp = Loop(nc, ctx, [f"x_in{i}" for i in range(MSTEP)] + [f"y_out{i}" for i in range(MSTEP)]
                  + ["x_ps", "x_turned", "h_ps", "h_sum", "h_act", "ht_ps", "ht_in", "y_ps", "y_sum"])
        ps, pair = m["ps"], m["pair"]
        with nc.Block() as block:
            @block.sync
            def _(sp):
                for k, dst, n in (("W1", W1, KC), ("W2", W2, FC)):
                    for c in range(n):
                        sp.dma_start(dst[:, c, :].rearrange("p (e f) -> p e f", e=E),
                                     w_dram[k][:, c * P:(c + 1) * P, :].rearrange("e p f -> p e f")).then_inc(load, 16)
                sp.dma_start(b1[:, :], w_dram["b1"].rearrange("e f -> (e f)").partition_broadcast(P)).then_inc(load, 16)
                sp.dma_start(b2[:, :], w_dram["b2"].rearrange("e f -> (e f)").partition_broadcast(P)).then_inc(load, 16)
                sp.wait_ge(load, 16 * (KC + FC + 2))
        with nc.Fori(0, MT // MSTEP) as r:
            with nc.Block(no_gpsimd_drain=True) as block:
                @block.sync
                def _(sp):
                    for s in range(MSTEP + NX):
                        if s < MSTEP:
                            if s >= NX:
                                sp.wait_ge(lp["x_ps"], s - NX + 1)
                            sp.dma_start(xs[:, s % NX, :], xs_dram[bass.ds((r * MSTEP + s) * P, P), :])\
                              .then_inc(lp[f"x_in{s}"], 16)
                        if s >= NX:
                            j = s - NX
                            sp.wait_ge(lp["y_sum"], j + 1)
                            sp.dma_start(ys_dram[bass.ds((r * MSTEP + j) * P, P), :], ys[:, j % 2, :])\
                              .then_inc(lp[f"y_out{j}"], 16)
                    for j in range(MSTEP):
                        sp.wait_ge(lp[f"y_out{j}"], 16)

                @block.tensor
                def _(pe):
                    e = [None] * MSTEP

                    def turn_in(j):
                        pe.wait_ge(lp[f"x_in{j}"], 16)
                        if j >= 1:
                            pe.wait_ge(lp["x_turned"], j)
                        for c in range(KC):
                            last = pe.transpose(ps[0][:, c * P:(c + 1) * P], xs[:, j % NX, c * P:(c + 1) * P],
                                                m["idf"][:, :])
                        last.then_inc(lp["x_ps"], 1)

                    def up(j):
                        e[j] = pe.value_load(g["expert"][0:1, bass.ds(r * MSTEP + j, 1)], min_val=0, max_val=E - 1)
                        pe.wait_ge(lp["x_turned"], j + 1)
                        if j >= 2:
                            pe.wait_ge(lp["h_sum"], j - 1)
                        for c in range(KC):
                            last = pe.matmul(pair[0][:, (j % 2) * F:(j % 2 + 1) * F], xsT[:, j % 2, c * P:(c + 1) * P],
                                             W1[:, c, bass.ts(e[j], F)], start=(c == 0), stop=(c == KC - 1))
                        last.then_inc(lp["h_ps"], 1)

                    def turn_h(j):
                        pe.wait_ge(lp["h_act"], j + 1)
                        if j >= 2:
                            pe.wait_ge(lp["ht_in"], j - 1)
                        for c in range(FC):
                            last = pe.transpose(ps[1 + j % 2][:, c * P:(c + 1) * P], hg[:, j % 2, c * P:(c + 1) * P],
                                                m["idf"][:, :])
                        last.then_inc(lp["ht_ps"], 1)

                    def down(j):
                        pe.wait_ge(lp["ht_in"], j + 1)
                        if j >= 2:
                            pe.wait_ge(lp["y_sum"], j - 1)
                        for c in range(FC):
                            last = pe.matmul(pair[1][:, (j % 2) * F:(j % 2) * F + D], hT[:, j % 2, c * P:(c + 1) * P],
                                             W2[:, c, bass.ts(e[j], D)], start=(c == 0), stop=(c == FC - 1))
                        last.then_inc(lp["y_ps"], 1)

                    turn_in(0)
                    for s in range(MSTEP + 2):
                        if s < MSTEP:
                            up(s)
                        if s + 1 < MSTEP:
                            turn_in(s + 1)
                        if 1 <= s < MSTEP + 1:
                            turn_h(s - 1)
                        if s >= 2:
                            down(s - 2)

                @block.scalar
                def _(act):
                    for s in range(MSTEP + 1):
                        if s < MSTEP:
                            act.wait_ge(lp["x_ps"], s + 1)
                            if s >= 2:
                                act.wait_ge(lp["h_ps"], s - 1)
                            act.activation(xsT[:, s % 2, :], ps[0][:, 0:D], ACT.Copy).then_inc(lp["x_turned"], 1)
                        if s >= 1:
                            j = s - 1
                            act.wait_ge(lp["h_sum"], j + 1)
                            if j >= 2:
                                act.wait_ge(lp["ht_ps"], j - 1)
                            act.activation(hg[:, j % 2, :], h[:, j % 2, :], ACT.Gelu).then_inc(lp["h_act"], 1)

                @block.vector
                def _(dve):
                    e = [None] * MSTEP
                    for s in range(MSTEP + 2):
                        if s < MSTEP:
                            e[s] = dve.value_load(g["expert"][0:1, bass.ds(r * MSTEP + s, 1)], min_val=0,
                                                  max_val=E - 1)
                            dve.wait_ge(lp["h_ps"], s + 1)
                            if s >= 2:
                                dve.wait_ge(lp["h_act"], s - 1)
                            dve.tensor_tensor(h[:, s % 2, :], pair[0][:, (s % 2) * F:(s % 2 + 1) * F],
                                              b1[:, bass.ts(e[s], F)], ALU.add).then_inc(lp["h_sum"], 1)
                        if 1 <= s < MSTEP + 1:
                            j = s - 1
                            dve.wait_ge(lp["ht_ps"], j + 1)
                            if j >= 2:
                                dve.wait_ge(lp["y_ps"], j - 1)
                            dve.tensor_copy(hT[:, j % 2, :], ps[1 + j % 2][:, :]).then_inc(lp["ht_in"], 1)
                        if s >= 2:
                            j = s - 2
                            dve.wait_ge(lp["y_ps"], j + 1)
                            if j >= 2:
                                dve.wait_ge(lp[f"y_out{j - 2}"], 16)
                            dve.tensor_tensor(ys[:, j % 2, :], pair[1][:, (j % 2) * F:(j % 2) * F + D],
                                              b2[:, bass.ts(e[j], D)], ALU.add).then_inc(lp["y_sum"], 1)

            lp.clear()


def layer1(nc, m, g, dram, ys_dram, out_dram):
    plan = Plan(causal=False)
    with ExitStack() as ctx:
        def sb(name, shape, dt=f32):
            return ctx.enter_context(nc.sbuf_tensor(name, shape, dt))

        bufs = attention_buffers(nc, ctx, "1", plan)
        w = {"qkv": sb("w_qkv", [P, KC, 3 * D]), "out": sb("w_out", [P, KC, D]), "rq": sb("w_rq", [P, KC, LD]),
             "rkv": sb("w_rkv", [P, KC, 2 * LD]), "rout": sb("w_rout", [2 * LD, D]),
             "wr": sb("w_router", [P, KC, E1]), "down": sb("w_down", [P, KC, E1 * F1]),
             "up": sb("w_up", [F1 + 1, E1 * D])}
        bias = {"qkv": sb("b_qkv", [P, 3 * D]), "rout": sb("b_rout", [P, D]), "out": sb("b_out", [P, D]),
                "br": sb("b_router", [P, E1]), "down": sb("b_down", [P, E1 * F1]),
                "ln_g": sb("ln_g", [P, D]), "ln_b": sb("ln_b", [P, D]), "gl": sb("gl", [P, HD]), "gr": sb("gr", [P, HD])}
        col = {"rq": sb("b_rq", [LD, 1]), "rkv": sb("b_rkv", [2 * LD, 1]), "bn_g": sb("bn_g", [P, KC]),
               "bn_b": sb("bn_b", [P, KC]), "bn_mean": sb("bn_mean", [P, KC]), "bn_var": sb("bn_var", [P, KC])}
        bn_rstd = sb("bn_rstd", [P, KC])
        yg, posb, scb = sb("gathered", [P, NT, D]), sb("place_b", [P, NT], u32), sb("score_b", [P, NT])
        xres, pooled, rkvT = sb("x_residual", [P, NT, D]), sb("pooled", [P, KC * LAT]), sb("rkvT", [P, LAT])
        BD, RVR, rqT = sb("block_diagonal", [P, LH, LAT]), sb("rv_rout", [P, 2 * D]), sb("rqT", [LD, S])
        R = sb("remote", [P, NT, D])
        lm, lsum, lrec = sb("latent_max", [P, NT * LH]), sb("latent_sum", [P, NT * LH]), sb("latent_rec", [P, NT * LH])
        spare = bufs["PT"][:, :, :, :].rearrange("p a h w -> p (a h w)")
        LS = spare[:, 0:NT * D].rearrange("p (t h l) -> p t h l", t=NT, h=LH)
        LT = spare[:, NT * D:2 * NT * D].rearrange("p (i s) -> p i s", i=2)
        u1, u2 = spare[:, 2 * NT * D:3 * NT * D], spare[:, 3 * NT * D:4 * NT * D]
        gs, ge = sb("gate_sum", [P, NT * H]), sb("gate_exp", [P, NT * H])
        zsum, zbn, zB = sb("z_sum", [P, KC]), sb("z_bn", [P, KC]), sb("z_bn_cols", [P, KC, P])
        rl, re, rsum, rgate = sb("router_logits", [P, E1]), sb("router_exp", [P, E1]), sb("router_sum", [P, 1]), sb("router_gate", [P, 1])
        rm, rw, idx = sb("router_max", [P, 1]), sb("router_which", [P, 1]), sb("router_idx", [P, 1], i32)
        hb, hT = sb("h_down", [P, NT, F1]), sb("h_downT", [F1 + 1, S])
        load = ctx.enter_context(nc.semaphore("layer1_weights"))
        ready = ctx.enter_context(nc.semaphore("buffers1"))
        first = ctx.enter_context(nc.semaphore("first_gather"))
        pre = ctx.enter_context(nc.semaphore("first_places"))
        bn = ctx.enter_context(nc.semaphore("bn_ready"))
        gathered = ctx.enter_context(nc.semaphore("gathered_ahead"))
        lp = Loop(nc, ctx, ATT + ["sc_in", "y_read", "places", "xres", "pooled", "rkv_ps", "rkv_in", "bd",
                                  "rvr_ps", "rvr_in", "rq_ps", "rq_in", "ls_ps", "l_sub", "l_exp", "l_p", "lt_ps",
                                  "lt_in", "r_ps", "r_in", "u_part", "g_sum", "g_exp", "mixed", "z", "z_ps", "z_in",
                                  "zb", "rl_ps", "rl", "r_exp", "idx", "h_ps", "h_in", "ht_ps", "ht_in", "u_ps",
                                  "stored"])
        at = Attention(nc, ctx, plan, m, lp, bufs)
        x_all, xb, y, xn, xT, A = g["x_all"], at.xb, at.y, at.xn, at.xT, at.A
        ps, pair = m["ps"], m["pair"]

        def gather(pool, sem):
            for t in range(NT):
                pool.indirect_dma_start(yg[:, t, :], None, ys_dram,
                                        bass.IndirectOffsetOnAxis(ap=posb[:, t:t + 1], axis=0)).then_inc(sem, 16)

        with nc.Block() as block:
            @block.sync
            def _(sp):
                n = 0

                def get(dst, src):
                    nonlocal n
                    sp.dma_start(dst, src).then_inc(load, 16)
                    n += 16

                for k in ("qkv", "out", "rq", "rkv", "wr"):
                    get(w[k][:, :, :], dram[k].rearrange("(c p) n -> p c n", p=P))
                get(w["rout"][0:LD, :], dram["rout"])
                get(w["rout"][LD:2 * LD, :], dram["rout"])
                for c in range(KC):
                    get(w["down"][:, c, :].rearrange("p (e f) -> p e f", e=E1),
                        dram["down"][:, c * P:(c + 1) * P, :].rearrange("e p f -> p e f"))
                get(w["up"][0:F1, :].rearrange("p (e d) -> p e d", e=E1), dram["up"].rearrange("e p d -> p e d"))
                get(w["up"][F1:F1 + 1, :], dram["b_up"].rearrange("(o n) -> o n", o=1))
                for k in ("qkv", "rout", "out", "br", "down", "ln_g", "ln_b", "gl", "gr"):
                    get(bias[k][:, :], dram["b_" + k].partition_broadcast(P))
                get(col["rq"][:, :], dram["c_rq"].rearrange("(p o) -> p o", o=1))
                get(col["rkv"][:, :], dram["c_rkv"].rearrange("(p o) -> p o", o=1))
                for k in ("bn_g", "bn_b", "bn_mean", "bn_var"):
                    for c in range(KC):
                        get(col[k][:, c:c + 1], dram[k][c * P:(c + 1) * P].rearrange("(p o) -> p o", o=1))
                sp.wait_ge(load, n)

            @block.vector
            def _(dve):
                start_buffers(dve, bufs, ready)
                dve.memset(hT[F1:F1 + 1, :], 1.0)
                dve.tensor_copy(posb[:, :], g["place"][:, 0:NT]).then_inc(pre, 1)

            @block.gpsimd
            def _(pool):
                pool.wait_ge(pre, 1)
                gather(pool, first)
                pool.wait_ge(first, 16 * NT)

        with nc.Block() as block:
            @block.gpsimd
            def _(pool):
                pool.tensor_scalar(bn_rstd[:, :], col["bn_var"][:, :], EPS, 1.0, ALU.add, ALU.mult).then_inc(bn, 1)
                pool.wait_ge(bn, 1)
                pool.tensor_tensor(bn_rstd[:, :], bn_rstd[:, :], m["half"][:, 0:KC], ALU.pow).then_inc(bn, 1)
                pool.wait_ge(bn, 2)
                pool.tensor_tensor(bn_rstd[:, :], bn_rstd[:, :], col["bn_g"][:, :], ALU.mult).then_inc(bn, 1)

        with nc.Fori(0, B) as b:
            with nc.Block(no_gpsimd_drain=True) as block:
                @block.sync
                def _(sp):
                    at.sp_maxima(sp)
                    sp.wait_ge(lp["x_new"], 4 * NT)
                    sp.dma_start(out_dram[bass.ds(b, 1), :, :].rearrange("o (t p) c -> p (o t) c", p=P), xn[:, :, :])\
                      .then_inc(lp["stored"], 16)
                    sp.wait_ge(lp["stored"], 16)

                @block.tensor
                def _(pe):
                    pe.wait_ge(lp["x_new"], NT)
                    at.pe_turn_x(pe, xb)
                    pe.wait_ge(lp["xt_act"], 1)
                    pe.wait_ge(lp["xt_dve"], 1)
                    pe.wait_ge(lp["pooled"], 1)
                    for c in range(KC):
                        last = pe.matmul(ps[2][:, 0:LAT], w["rkv"][:, c, :], pooled[:, c * LAT:(c + 1) * LAT],
                                         start=(c == 0), stop=(c == KC - 1))
                    last.then_inc(lp["rkv_ps"], 1)
                    for c in range(KC):
                        last = pe.matmul(ps[0][0:LD, :], w["rq"][:, c, :], xT[:, c, :],
                                         start=(c == 0), stop=(c == KC - 1))
                    last.then_inc(lp["rq_ps"], 1)
                    pe.wait_ge(lp["bd"], 1)
                    for i in range(2):
                        last = pe.matmul(ps[3][:, i * D:(i + 1) * D],
                                         BD[LD:2 * LD, 2 * i:2 * i + 2, :].rearrange("p h l -> p (h l)"),
                                         w["rout"][LD:2 * LD, :], start=True, stop=True)
                    last.then_inc(lp["rvr_ps"], 1)
                    pe.wait_ge(lp["rq_in"], 1)
                    for t in range(NT):
                        last = pe.matmul(pair[0][:, t * D:(t + 1) * D], rqT[:, t * P:(t + 1) * P],
                                         BD[0:LD, :, :].rearrange("p h l -> p (h l)"), start=True, stop=True)
                    last.then_inc(lp["ls_ps"], 1)
                    pe.wait_ge(lp["l_p"], 1)
                    for i in range(2):
                        for t in range(NT):
                            last = pe.transpose(pair[1][:, i * S + t * P:i * S + (t + 1) * P],
                                                LS[:, t, 2 * i:2 * i + 2, :].rearrange("p h l -> p (h l)"),
                                                m["idf"][:, :])
                    last.then_inc(lp["lt_ps"], 1)
                    pe.wait_ge(lp["lt_in"], 1)
                    pe.wait_ge(lp["rvr_in"], 1)
                    for t in range(NT):
                        for i in range(2):
                            last = pe.matmul(pair[0][:, t * D:(t + 1) * D], LT[:, i, t * P:(t + 1) * P],
                                             RVR[:, i * D:(i + 1) * D], start=(i == 0), stop=(i == 1))
                    last.then_inc(lp["r_ps"], 1)
                    pe.wait_ge(lp["r_in"], 1)
                    at.pe_tiles(pe, w["qkv"])
                    at.pe_attend(pe)
                    at.pe_turn_o(pe)
                    pe.wait_ge(lp["mixed"], 1)
                    at.pe_out(pe, A, w["out"])
                    pe.wait_ge(lp["z"], 1)
                    for c in range(KC):
                        for t in range(NT):
                            last = pe.transpose(pair[0][:, c * S + t * P:c * S + (t + 1) * P],
                                                y[:, t, c * P:(c + 1) * P], m["idf"][:, :])
                    last.then_inc(lp["z_ps"], 1)
                    pe.wait_ge(lp["zb"], 1)
                    for c in range(KC):
                        last = pe.matmul(ps[0][:, 0:E1], zB[:, c, :], w["wr"][:, c, :],
                                         start=(c == 0), stop=(c == KC - 1))
                    last.then_inc(lp["rl_ps"], 1)
                    pe.wait_ge(lp["idx"], 1)
                    e = pe.value_load(idx[0:1, 0:1], min_val=0, max_val=E1 - 1)
                    for t in range(NT):
                        for c in range(KC):
                            last = pe.matmul(ps[1][:, t * F1:(t + 1) * F1], xT[:, c, t * P:(t + 1) * P],
                                             w["down"][:, c, bass.ts(e, F1)], start=(c == 0), stop=(c == KC - 1))
                    last.then_inc(lp["h_ps"], 1)
                    pe.wait_ge(lp["h_in"], 1)
                    for t in range(NT):
                        last = pe.transpose(ps[2][0:F1, t * P:(t + 1) * P], hb[:, t, :], m["idf"][:, :])
                    last.then_inc(lp["ht_ps"], 1)
                    pe.wait_ge(lp["ht_in"], 1)
                    for t in range(NT):
                        last = pe.matmul(pair[1][:, t * D:(t + 1) * D], hT[:, t * P:(t + 1) * P],
                                         w["up"][:, bass.ts(e, D)], start=True, stop=True)
                    last.then_inc(lp["u_ps"], 1)

                @block.scalar
                def _(act):
                    act.wait_ge(lp["xt_ps"], 1)
                    act.activation(xT[:, 0, :], ps[0][:, :], ACT.Copy).then_inc(lp["xt_act"], 1)
                    act.wait_ge(lp["rkv_ps"], 1)
                    act.activation(rkvT[:, :], ps[2][:, 0:LAT], ACT.Identity, bias=col["rkv"][:, 0:1],
                                   scale=1.0 / CH).then_inc(lp["rkv_in"], 1)
                    act.wait_ge(lp["rq_ps"], 1)
                    act.activation(rqT[:, :], ps[0][0:LD, :], ACT.Identity, bias=col["rq"][:, 0:1])\
                       .then_inc(lp["rq_in"], 1)
                    act.wait_ge(lp["rvr_ps"], 1)
                    act.activation(RVR[:, :], ps[3][:, :], ACT.Copy).then_inc(lp["rvr_in"], 1)
                    act.wait_ge(lp["l_sub"], 1)
                    act.activation(LS[:, :, :, :], LS[:, :, :, :], ACT.Exp, scale=SCALE).then_inc(lp["l_exp"], 1)
                    act.wait_ge(lp["lt_ps"], 1)
                    act.activation(LT[:, :, :], pair[1][:, :].rearrange("p (i s) -> p i s", i=2), ACT.Copy)\
                       .then_inc(lp["lt_in"], 1)
                    for s in range(NT + 2):
                        if s < NT:
                            at.act_tile(act, s)
                        if s >= 2:
                            at.act_stacks(act, s - 2)
                    at.act_attend(act)
                    act.wait_ge(lp["g_sum"], 1)
                    act.activation(ge[:, :], gs[:, :], ACT.Exp).then_inc(lp["g_exp"], 1)
                    act.wait_ge(lp["a_ps"], 1)
                    act.activation(xT[:, 0, :], pair[0][:, 0:S], ACT.Copy).then_inc(lp["at_act"], 1)
                    act.wait_ge(lp["z_ps"], 1)
                    for c in range(KC):
                        act.activation(xT[:, c, :], pair[0][:, c * S:(c + 1) * S], ACT.Copy,
                                       accum_out=zsum[:, c:c + 1]).then_inc(lp["z_in"], 1)
                    act.wait_ge(lp["rl"], 1)
                    act.activation(re[:, :], rl[:, :], ACT.Exp, accum_out=rsum[:, 0:1]).then_inc(lp["r_exp"], 1)
                    act.wait_ge(lp["ht_ps"], 1)
                    act.activation(hT[0:F1, :], ps[2][0:F1, :], ACT.Copy).then_inc(lp["ht_in"], 1)

                @block.gpsimd
                def _(pool):
                    pool.wait_ge(lp["places"], 1)
                    pool.wait_ge(lp["y_read"], NT)
                    gather(pool, gathered)
                    pool_rstd(pool, lp, at.ve[:, :], at.rstd[:, :], m["half"][:, :], 1)
                    pool.wait_ge(lp["x_new"], NT)
                    pool.tensor_tensor(xres[:, :, :], xb[:, :, :], spread(bias["out"][:, :], D, NT), ALU.add)\
                        .then_inc(lp["xres"], 1)
                    for s in range(NT):
                        at.pool_part2(pool, s)
                    pool.wait_ge(lp["pv_ps"], NG)
                    pool.tensor_tensor(u2[:, :].rearrange("p (n c) -> p n c", c=HD),
                                       R[:, :, :].rearrange("p t (h c) -> p (t h) c", c=HD),
                                       spread(bias["gr"][:, :], HD, NT * H), ALU.mult).then_inc(lp["u_part"], 1)
                    pool.wait_ge(lp["a_norm"], NT)
                    pool.tensor_tensor(u1[:, :].rearrange("p (n c) -> p n c", c=HD),
                                       A[:, :, :].rearrange("p t (h c) -> p (t h) c", c=HD),
                                       spread(bias["gl"][:, :], HD, NT * H), ALU.mult).then_inc(lp["u_part"], 1)
                    for n in (2, 3, 4):
                        pool_rstd(pool, lp, at.ve[:, :], at.rstd[:, :], m["half"][:, :], n)
                    pool.wait_ge(gathered, (b + 1) * (16 * NT))

                @block.vector
                def _(dve):
                    ch = Chain(dve, lp["dve_chain"])

                    def step(ins):
                        ch.step(ins)
                        ch.settle()

                    def norm(out, turn):
                        dve_layernorm(dve, lp, ch, y, at.mv, at.st, at.ve[:, :], at.rstd, out, turn)

                    dve.tensor_copy(scb[:, :], g["score"][:, bass.ts(b, NT)]).then_inc(lp["sc_in"], 1)
                    dve.wait_ge(lp["sc_in"], 1)
                    dve.tensor_copy(posb[:, :], g["place"][:, bass.ds(b * NT + NT, NT)]).then_inc(lp["places"], 1)
                    for t in range(NT):
                        dve.scalar_tensor_tensor(out=y[:, t, :], in0=yg[:, t, :], scalar=scb[:, t:t + 1],
                                                 in1=x_all[:, bass.ds(b * NT + t, 1), :].rearrange("p o c -> p (o c)"),
                                                 op0=ALU.mult, op1=ALU.add).then_inc(lp["y_read"], 1)
                    dve.wait_ge(lp["y_read"], NT)
                    norm(xb, 1)
                    dve.wait_ge(lp["xt_ps"], 2)
                    dve.tensor_copy(xT[:, 1, :], ps[1][:, :]).then_inc(lp["xt_dve"], 1)
                    dve.wait_ge(lp["xt_dve"], 1)
                    dve.wait_ge(lp["xt_act"], 1)
                    dve.tensor_reduce(pooled[:, :], xT[:, :, :].rearrange("p c (l k) -> p (c l) k", k=CH),
                                      AX.X, ALU.add).then_inc(lp["pooled"], 1)
                    dve.wait_ge(lp["rkv_in"], 1)
                    dve.tensor_tensor(BD[:, :, :], spread(rkvT[:, :], LAT, LH),
                                      m["heads"][:, :].rearrange("p (h o) -> p h o", o=1).to_broadcast([P, LH, LAT]),
                                      ALU.mult).then_inc(lp["bd"], 1)
                    dve.wait_ge(lp["ls_ps"], 1)
                    for i in range(2):
                        ch.step(dve.tensor_tensor(
                            LS[:, 2 * i:2 * i + 2, :, :],
                            pair[0][:, i * S:(i + 1) * S].rearrange("p (t h l) -> p t h l", t=2, h=LH),
                            m["lat"][:, 2 * i * LAT:(2 * i + 2) * LAT].rearrange("p (t o l) -> p t o l", t=2, o=1)
                                      .to_broadcast([P, 2, LH, LAT]), ALU.add))
                    ch.settle()
                    flat = LS[:, :, :, :].rearrange("p t h l -> p (t h) l")

                    def over(ap):
                        return ap.rearrange("p (n o) -> p n o", o=1).to_broadcast([P, NT * LH, LAT])

                    step(dve.tensor_reduce(lm[:, :], flat, AX.X, ALU.max, negate=True))
                    step(dve.tensor_scalar(lm[:, :], lm[:, :], -NEG / 10, None, ALU.min))
                    dve.tensor_tensor(flat, flat, over(lm[:, :]), ALU.add).then_inc(lp["l_sub"], 1)
                    dve.wait_ge(lp["l_exp"], 1)
                    step(dve.tensor_reduce(lsum[:, :], flat, AX.X, ALU.add))
                    step(dve.tensor_scalar(lsum[:, :], lsum[:, :], -1.0 / NEG, None, ALU.max))
                    step(dve.reciprocal(lrec[:, :], lsum[:, :]))
                    dve.tensor_tensor(flat, flat, over(lrec[:, :]), ALU.mult).then_inc(lp["l_p"], 1)
                    dve.wait_ge(lp["r_ps"], 1)
                    dve.tensor_tensor(R[:, :, :], pair[0][:, :].rearrange("p (t c) -> p t c", c=D),
                                      spread(bias["rout"][:, :], D, NT), ALU.add).then_inc(lp["r_in"], 1)
                    for s in range(NT + 3):
                        if s < NT:
                            dve.wait_ge(lp["qk_ps"], s + 1)
                            if s >= 2:
                                dve.wait_ge(lp["part1"], s - 1)
                                dve.wait_ge(lp["rest1"], s - 1)
                            dve.tensor_tensor(at.qk[:, s % 2, :], pair[s % 2][:, 0:2 * D], bias["qkv"][:, 0:2 * D],
                                              ALU.add).then_inc(lp["qk_read"], 1)
                            dve.wait_ge(lp["v_ps"], s + 1)
                            dve.tensor_tensor(at.V[:, s, :, 0:HD],
                                              pair[s % 2][:, 2 * D:3 * D].rearrange("p (h c) -> p h c", c=HD),
                                              bias["qkv"][:, 2 * D:3 * D].rearrange("p (h c) -> p h c", c=HD),
                                              ALU.add).then_inc(lp["v_in"], 1)
                        if 2 <= s < NT + 2:
                            at.dve_part3(dve, s - 2)
                        if 1 <= s < NT + 1:
                            at.dve_rest1(dve, s - 1)
                        if s >= 3:
                            at.dve_stacks(dve, s - 3)
                    at.dve_attend(dve, ch)
                    at.dve_normalise(dve, ch)
                    Af, Rf = A[:, :, :].rearrange("p t c -> p (t c)"), R[:, :, :].rearrange("p t c -> p (t c)")
                    dve.wait_ge(lp["u_part"], 2)
                    step(dve.tensor_tensor(u1[:, :], u1[:, :], u2[:, :], ALU.add))
                    dve.tensor_reduce(gs[:, :], u1[:, :].rearrange("p (n c) -> p n c", c=HD), AX.X, ALU.add,
                                      negate=True).then_inc(lp["g_sum"], 1)
                    step(dve.tensor_tensor(Af, Af, Rf, ALU.subtract))
                    dve.wait_ge(lp["g_exp"], 1)
                    step(dve.tensor_scalar(ge[:, :], ge[:, :], 1.0, None, ALU.add))
                    step(dve.reciprocal(gs[:, :], ge[:, :]))
                    step(dve.tensor_tensor(Af.rearrange("p (n c) -> p n c", c=HD),
                                           Af.rearrange("p (n c) -> p n c", c=HD),
                                           gs[:, :].rearrange("p (n o) -> p n o", o=1).to_broadcast([P, NT * H, HD]),
                                           ALU.mult))
                    dve.tensor_tensor(Af, Af, Rf, ALU.add).then_inc(lp["mixed"], 1)
                    dve.wait_ge(lp["a_ps"], 2)
                    dve.tensor_copy(xT[:, 1, :], pair[0][:, S:2 * S]).then_inc(lp["at_dve"], 1)
                    dve.wait_ge(lp["xres"], 1)
                    for i in range(2):
                        dve.wait_ge(lp["y_ps"], i + 1)
                        dve.tensor_tensor(y[:, 2 * i:2 * i + 2, :], pair[1][:, i * S:(i + 1) * S]
                                          .rearrange("p (t c) -> p t c", c=D), xres[:, 2 * i:2 * i + 2, :],
                                          ALU.add).then_inc(lp["y_in"], 1)
                    dve.wait_ge(lp["y_in"], 2)
                    norm(xb, 2)
                    dve.wait_ge(lp["x_new"], 2 * NT)
                    for t in range(NT):
                        ch.step(dve.bn_stats(at.st[:, t, :], xb[:, t, :]))
                    ch.settle()
                    for t in range(NT):
                        ch.step(dve.bn_aggr(at.mv[:, t, :], at.st[:, t, :]))
                    ch.settle()
                    dve.tensor_scalar(at.ve[:, :], at.mv[:, :, 1], EPS, None, ALU.add).then_inc(lp["var"], 1)
                    dve.wait_ge(lp["rstd"], 3)
                    for t in range(NT):
                        dve.tensor_scalar(y[:, t, :], xb[:, t, :], at.mv[:, t, 0:1], at.rstd[:, t:t + 1],
                                          ALU.subtract, ALU.mult).then_inc(lp["x_new"], 1)
                    dve.wait_ge(lp["x_new"], 3 * NT)
                    step(dve.tensor_tensor(y[:, :, :], y[:, :, :], spread(bias["ln_g"][:, :], D, NT), ALU.mult))
                    dve.tensor_tensor(y[:, :, :], y[:, :, :], spread(bias["ln_b"][:, :], D, NT), ALU.add)\
                        .then_inc(lp["z"], 1)
                    dve.wait_ge(lp["z_in"], KC)
                    step(dve.tensor_scalar(zbn[:, :], zsum[:, :], 1.0 / S, None, ALU.mult))
                    step(dve.tensor_tensor(zbn[:, :], zbn[:, :], col["bn_mean"][:, :], ALU.subtract))
                    step(dve.tensor_tensor(zbn[:, :], zbn[:, :], bn_rstd[:, :], ALU.mult))
                    step(dve.tensor_tensor(zbn[:, :], zbn[:, :], col["bn_b"][:, :], ALU.add))
                    dve.tensor_copy(zB[:, :, :], zbn[:, :].rearrange("p (c o) -> p c o", o=1)
                                    .to_broadcast([P, KC, P])).then_inc(lp["zb"], 1)
                    dve.wait_ge(lp["rl_ps"], 1)
                    step(dve.tensor_tensor(rl[:, :], ps[0][:, 0:E1], bias["br"][:, :], ALU.add))
                    step(dve.tensor_reduce(rm[:, :], rl[:, :], AX.X, ALU.max, negate=True))
                    dve.tensor_scalar(rl[:, :], rl[:, :], rm[:, 0:1], None, ALU.add).then_inc(lp["rl"], 1)
                    dve.wait_ge(lp["r_exp"], 1)
                    step(dve.reciprocal(rgate[:, :], rsum[:, :]))
                    step(dve.tensor_scalar(re[:, :], rl[:, :], 0.0, None, ALU.is_equal))
                    step(dve.tensor_tensor(re[:, :], re[:, :], m["less"][:, :], ALU.mult))
                    step(dve.tensor_reduce(rw[:, :], re[:, :], AX.X, ALU.min))
                    dve.tensor_scalar(idx[:, :], rw[:, :], float(E1), None, ALU.add).then_inc(lp["idx"], 1)
                    dve.wait_ge(lp["idx"], 1)
                    e = dve.value_load(idx[0:1, 0:1], min_val=0, max_val=E1 - 1)
                    dve.wait_ge(lp["h_ps"], 1)
                    step(dve.tensor_tensor(hb[:, :, :], ps[1][:, 0:NT * F1].rearrange("p (t f) -> p t f", f=F1),
                                           spread(bias["down"][:, bass.ts(e, F1)], F1, NT), ALU.add))
                    dve.tensor_scalar(hb[:, :, :], hb[:, :, :], 0.0, None, ALU.max).then_inc(lp["h_in"], 1)
                    dve.wait_ge(lp["u_ps"], 1)
                    step(dve.scalar_tensor_tensor(out=y[:, :, :], in0=pair[1][:, :].rearrange("p (t c) -> p t c", c=D),
                                                  scalar=rgate[:, 0:1],
                                                  in1=xb[:, :, :], op0=ALU.mult, op1=ALU.add))
                    norm(xn, 4)
            lp.clear()


def program(nc, a, out):
    with ExitStack() as ctx:
        def sb(name, shape, dt=f32):
            return ctx.enter_context(nc.sbuf_tensor(name, shape, dt))

        xs_dram = nc.dram_tensor("sorted_x", [MT * P, D], f32, kind="Internal").ap()
        ys_dram = nc.dram_tensor("sorted_y", [MT * P, D], f32, kind="Internal").ap()
        width = sum(CONST.values())
        cst, casts = sb("constants", [P, width]), sb("constants_bf", [P, CASTS], bf16)
        at, m = 0, {}
        for k, n in CONST.items():
            m[k] = (casts if at + n <= CASTS and k != "id" else cst)[:, at:at + n]
            if k == "id":
                m["idf"], m["idb"] = cst[:, at:at + n], casts[:, at:at + n]
            at += n
        m["half"] = sb("minus_half", [P, NT])
        g = {"x_all": sb("x_all", [P, TILES, D]), "logits": sb("logits", [P, TILES, E]),
             "score": sb("score", [P, TILES]), "place": sb("place", [P, TILES + NT], u32),
             "expert": sb("expert", [P, MT + 1], i32)}
        m["ps"] = [ctx.enter_context(nc.psum_tensor(f"bank{i}", [P, S], f32)) for i in range(4)]
        m["pair"] = [ctx.enter_context(nc.psum_tensor(f"pair{i}", [P, 2 * S], f32)) for i in range(2)]
        load = ctx.enter_context(nc.semaphore("loaded"))
        with ExitStack() as inner:
            def si(name, shape, dt=f32):
                return inner.enter_context(nc.sbuf_tensor(name, shape, dt))

            w = {"qkv0": si("w_qkv0", [P, KC, 3 * D]), "o0": si("w_o0", [P, KC, D]), "red": si("w_red", [P, KC, G0]),
                 "gT": si("wg_T", [G0, E])}
            wg, sq, nrm = si("wg", [E, G0]), si("wg_squares", [E, G0]), si("wg_norm", [E, 2])
            zero = si("zero", [P, MSTEP * D])
            root = si("plus_half", [E, 1])
            steps = inner.enter_context(nc.semaphore("setup_steps"))
            cleared = inner.enter_context(nc.semaphore("sorted_cleared"))
            zs = inner.enter_context(nc.semaphore("zero_set"))
            sqs = inner.enter_context(nc.semaphore("squares"))
            roots = inner.enter_context(nc.semaphore("roots"))
            turned = inner.enter_context(nc.semaphore("wg_turned"))
            normed = inner.enter_context(nc.semaphore("wg_normed"))
            with nc.Block() as block:
                @block.sync
                def _(sp):
                    n = 0
                    for dst, src in [(cst[:, :], a["const"]), (wg[:, :], a["wg"]),
                                     (w["qkv0"][:, :, :], a["qkv0"].rearrange("(c p) n -> p c n", p=P)),
                                     (w["o0"][:, :, :], a["o0"].rearrange("(c p) n -> p c n", p=P)),
                                     (w["red"][:, :, :], a["red"].rearrange("(c p) n -> p c n", p=P)),
                                     (g["x_all"][:, :, :], a["x"].rearrange("b (t p) c -> p (b t) c", p=P))]:
                        sp.dma_start(dst, src).then_inc(load, 16)
                        n += 16
                    sp.wait_ge(zs, 1)
                    rows = MSTEP * P
                    for i in range(MT // MSTEP):
                        sp.dma_start(xs_dram[i * rows:(i + 1) * rows, :].rearrange("(p n) c -> p (n c)", p=P),
                                     zero[:, :]).then_inc(cleared, 16)
                    sp.wait_ge(load, n)
                    sp.wait_ge(cleared, 16 * (MT // MSTEP))

                @block.vector
                def _(dve):
                    dve.memset(zero[:, :], 0.0).then_inc(zs, 1)
                    dve.memset(m["half"][:, :], -0.5)
                    dve.wait_ge(load, 96)
                    dve.tensor_copy(casts[:, :], cst[:, 0:CASTS])
                    dve.tensor_tensor(sq[:, :], wg[:, :], wg[:, :], ALU.mult).then_inc(steps, 1)
                    dve.wait_ge(steps, 1)
                    dve.tensor_reduce(nrm[:, 0:1], sq[:, :], AX.X, ALU.add).then_inc(sqs, 1)
                    dve.wait_ge(roots, 2)
                    dve.tensor_scalar(nrm[:, 0:1], nrm[:, 1:2], 1e-4, None, ALU.max).then_inc(steps, 1)
                    dve.wait_ge(steps, 2)
                    dve.reciprocal(nrm[:, 1:2], nrm[:, 0:1]).then_inc(steps, 1)
                    dve.wait_ge(steps, 3)
                    dve.tensor_scalar(sq[:, :], wg[:, :], nrm[:, 1:2], None, ALU.mult).then_inc(normed, 1)
                    dve.wait_ge(turned, 1)
                    dve.tensor_copy(w["gT"][:, :], m["ps"][0][0:G0, 0:E])

                @block.gpsimd
                def _(pool):
                    pool.memset(root[:, :], 0.5).then_inc(roots, 1)
                    pool.wait_ge(roots, 1)
                    pool.wait_ge(sqs, 1)
                    pool.tensor_tensor(nrm[:, 1:2], nrm[:, 0:1], root[:, :], ALU.pow).then_inc(roots, 1)

                @block.tensor
                def _(pe):
                    pe.wait_ge(normed, 1)
                    pe.transpose(m["ps"][0][0:G0, 0:E], sq[:, :], m["idf"][0:E, 0:E]).then_inc(turned, 1)
            layer0_attention(nc, m, g, w)
        route(nc, m, g, xs_dram)
        experts(nc, m, g, {"W1": a["W1"], "W2": a["W2"], "b1": a["b1"], "b2": a["b2"]}, xs_dram, ys_dram)
        layer1(nc, m, g, a, ys_dram, out)


def constants():
    import numpy as np
    i, j = np.arange(P)[:, None], np.arange(P)[None, :]

    def mask(allowed):
        return np.where(allowed, 0.0, NEG)

    inv = (1.0 / 10000.0 ** (np.arange(0, HD, 2, dtype=np.float32) / np.float32(HD))).astype(np.float32)
    ang = np.repeat(np.arange(S, dtype=np.float32)[:, None] * inv[None, :], 2, axis=-1)
    sign = np.where(np.arange(HD) % 2 == 0, -1.0, 1.0)

    def table(x):
        return x.reshape(NT, P, HD).transpose(1, 0, 2).reshape(P, NT * HD)

    prev = (j >= i) & (i + j > 0)
    nxt = (i >= j) & (i + j > 0)
    tok = (np.arange(NT)[:, None] * P + np.arange(P)[None, :]) // CH
    lat = mask(np.arange(LAT)[None, None, :] < tok.T[:, :, None]).reshape(P, NT * LAT)
    parts = {
        "id": i == j, "mS0": mask(j <= i), "mT0": mask(i <= j),
        "mS1": np.concatenate([mask(prev), mask(j < i)], 1), "mT1": np.concatenate([mask(i < j), mask(nxt)], 1),
        "tri": i < j, "cos": table(np.cos(ang)), "sin": table(np.sin(ang) * sign), "lat": lat,
        "heads": (i % LD) // HD == np.arange(LH)[None, :], "less": np.broadcast_to(np.arange(E) - float(E), (P, E)),
    }
    assert {k: v.shape[1] for k, v in parts.items()} == CONST
    return np.ascontiguousarray(np.concatenate([np.asarray(parts[k], np.float32) for k in CONST], 1))


def kernel(**x):
    import numpy as np
    import concourse.bacc as bacc
    from concourse.bass_utils import run_bass_kernel_spmd

    x = {k: np.asarray(v) for k, v in x.items()}
    arrays = {
        "const": constants(), "x": x["L0_attn_x"],
        "qkv0": np.concatenate([x["L0_attn_Wq"].T, x["L0_attn_Wk"].T, x["L0_attn_Wv"].T], 1), "o0": x["L0_attn_Wo"].T,
        "red": x["L0_ffn_w_red"], "wg": x["L0_ffn_wg"], "W1": x["L0_ffn_W1"], "b1": x["L0_ffn_b1"],
        "W2": x["L0_ffn_W2"], "b2": x["L0_ffn_b2"],
        "qkv": x["L1_attn_qkv_w"], "b_qkv": x["L1_attn_qkv_b"], "rq": x["L1_attn_rq_w"], "c_rq": x["L1_attn_rq_b"],
        "rkv": x["L1_attn_rkv_w"], "c_rkv": x["L1_attn_rkv_b"], "rout": x["L1_attn_rout_w"],
        "b_rout": x["L1_attn_rout_b"], "out": x["L1_attn_out_w"], "b_out": x["L1_attn_out_b"],
        "b_gl": x["L1_attn_gl_w"].reshape(-1), "b_gr": x["L1_attn_gr_w"].reshape(-1),
        "b_ln_g": x["L1_ffn_ln_g"], "b_ln_b": x["L1_ffn_ln_b"], "bn_g": x["L1_ffn_bn_g"], "bn_b": x["L1_ffn_bn_b"],
        "bn_mean": x["L1_ffn_bn_mean"], "bn_var": x["L1_ffn_bn_var"], "wr": x["L1_ffn_Wr"], "b_br": x["L1_ffn_br"],
        "down": x["L1_ffn_W_down"], "b_down": x["L1_ffn_b_down"].reshape(-1), "up": x["L1_ffn_W_up"],
        "b_up": x["L1_ffn_b_up"].reshape(-1),
    }
    arrays = {f"in_{k}": np.ascontiguousarray(v) for k, v in arrays.items()}
    nc = bacc.Bacc("TRN2", target_bir_lowering=False, num_devices=1)
    a = {k[3:]: nc.dram_tensor(k, v.shape, mybir.dt.from_np(v.dtype), kind="ExternalInput").ap()
         for k, v in arrays.items()}
    out = nc.dram_tensor("out", (B, S, D), f32, kind="ExternalOutput").ap()
    program(nc, a, out)
    return run_bass_kernel_spmd(nc, [arrays], core_ids=[0]).results[0]["out"]
```
